# Optimizing a Trainium2 kernel written in Bass

```python
import numpy as np
import jax
import jax.numpy as jnp

def _softmax(x, axis=-1):
    return jax.nn.softmax(x, axis=axis)

def _gelu(x):
    return jax.nn.gelu(x, approximate=True)

def _silu(x):
    return jax.nn.silu(x)

def _sigmoid(x):
    return jax.nn.sigmoid(x)

def _layernorm(x, axis=-1, eps=1e-05):
    m = jnp.mean(x, axis=axis, keepdims=True)
    v = jnp.var(x, axis=axis, keepdims=True)
    return (x - m) / jnp.sqrt(v + eps)

def _scatter_add(tgt, idx, src, axis=0):
    return tgt.at[idx].add(src)

def _segment_sum(src, seg, n):
    return jax.ops.segment_sum(src, seg, n)
kernel_name = 'mk_seq_preln_d1_jaxref_r4_102af7'

def setup_inputs(seed: int=0):
    np.random.seed(seed)
    _w = jnp.asarray

    def _L0_attn_setup():
        import jax, jax.numpy as jnp
        import numpy as np
        EMB = 256
        HEADS = 16
        HEAD_DIM = EMB // HEADS
        BLOCK = 64
        N_GLOBAL = 4
        WINDOW = 128
        ROPE_BASE = 10000.0

        def rotate_half(x):
            x1 = x[..., ::2]
            x2 = x[..., 1::2]
            return jnp.stack((-x2, x1), axis=-1).reshape(x.shape)

        def rope_cos_sin(seq_len, dtype=jnp.float32):
            inv_freq = 1.0 / ROPE_BASE ** (jnp.arange(0, HEAD_DIM, 2, dtype=jnp.float32) / HEAD_DIM)
            pos = jnp.arange(seq_len, dtype=jnp.float32)
            freqs = jnp.outer(pos, inv_freq)
            emb = jnp.concatenate([freqs, freqs], -1)
            return (jnp.cos(emb)[None, None].astype(dtype), jnp.sin(emb)[None, None].astype(dtype))

        def block_mask(seq_len):
            i = jnp.arange(seq_len)[:, None]
            j = jnp.arange(seq_len)[None, :]
            blk = i // BLOCK == j // BLOCK
            glob = (i < N_GLOBAL) | (j < N_GLOBAL)
            slide = jnp.abs(i - j) <= WINDOW
            return (blk | glob | slide) & (j <= i)
        key = jax.random.key(seed)
        kx, kq, ko = jax.random.split(key, 3)
        B, S = (2, 512)
        x = jax.random.normal(kx, (B, S, EMB), jnp.float32)
        qkv_w = jax.random.normal(kq, (3 * EMB, EMB), jnp.float32) * EMB ** (-0.5)
        out_w = jax.random.normal(ko, (EMB, EMB), jnp.float32) * EMB ** (-0.5)
        return {'x': x, 'qkv_w': qkv_w, 'out_w': out_w}
    _L0_attn_in = _L0_attn_setup()

    def _L0_ffn_setup():
        import jax, jax.numpy as jnp
        import numpy as np
        D_IN, D_HID = (256, 1024)

        def _ternary(key, shape):
            return jax.random.randint(key, shape, -1, 2).astype(jnp.float32)

        def _tlin(x, w, s):
            return jnp.einsum('bsi,oi->bso', x, w) * s
        key = jax.random.key(seed)
        ks = jax.random.split(key, 12)
        inv = lambda fan: 1.0 / np.sqrt(fan).astype(np.float32)
        return {'x': jax.random.normal(ks[0], (4, 512, D_IN), dtype=jnp.float32), 'w1_w': _ternary(ks[1], (D_HID, D_IN)), 'w1_s': jax.random.uniform(ks[2], (D_HID,), dtype=jnp.float32) * inv(D_IN), 'w2_w': _ternary(ks[3], (D_HID, D_IN)), 'w2_s': jax.random.uniform(ks[4], (D_HID,), dtype=jnp.float32) * inv(D_IN), 'h1_w': _ternary(ks[5], (D_HID, D_HID)), 'h1_s': jax.random.uniform(ks[6], (D_HID,), dtype=jnp.float32) * inv(D_HID), 'h2_w': _ternary(ks[7], (D_HID, D_HID)), 'h2_s': jax.random.uniform(ks[8], (D_HID,), dtype=jnp.float32) * inv(D_HID), 'w3_w': _ternary(ks[9], (D_IN, D_HID)), 'w3_s': jax.random.uniform(ks[10], (D_IN,), dtype=jnp.float32) * inv(D_HID)}
    _L0_ffn_in = _L0_ffn_setup()
    _d = {'L0_attn_x': _L0_attn_in['x'], 'L0_attn_qkv_w': _L0_attn_in['qkv_w'], 'L0_attn_out_w': _L0_attn_in['out_w'], 'L0_ffn_w1_w': _L0_ffn_in['w1_w'], 'L0_ffn_w1_s': _L0_ffn_in['w1_s'], 'L0_ffn_w2_w': _L0_ffn_in['w2_w'], 'L0_ffn_w2_s': _L0_ffn_in['w2_s'], 'L0_ffn_h1_w': _L0_ffn_in['h1_w'], 'L0_ffn_h1_s': _L0_ffn_in['h1_s'], 'L0_ffn_h2_w': _L0_ffn_in['h2_w'], 'L0_ffn_h2_s': _L0_ffn_in['h2_s'], 'L0_ffn_w3_w': _L0_ffn_in['w3_w'], 'L0_ffn_w3_s': _L0_ffn_in['w3_s']}
    _x0 = _d['L0_attn_x']
    _d['L0_attn_x'] = jax.random.normal(jax.random.fold_in(jax.random.key(seed), 1), (8, 512, 256), dtype=_x0.dtype)
    del _x0
    return _d

def reference(L0_attn_x, L0_attn_qkv_w, L0_attn_out_w, L0_ffn_w1_w, L0_ffn_w1_s, L0_ffn_w2_w, L0_ffn_w2_s, L0_ffn_h1_w, L0_ffn_h1_s, L0_ffn_h2_w, L0_ffn_h2_s, L0_ffn_w3_w, L0_ffn_w3_s):

    def _L0_attn_ref(x, qkv_w, out_w):
        import jax, jax.numpy as jnp
        import numpy as np
        EMB = 256
        HEADS = 16
        HEAD_DIM = EMB // HEADS
        BLOCK = 64
        N_GLOBAL = 4
        WINDOW = 128
        ROPE_BASE = 10000.0

        def rotate_half(x):
            x1 = x[..., ::2]
            x2 = x[..., 1::2]
            return jnp.stack((-x2, x1), axis=-1).reshape(x.shape)

        def rope_cos_sin(seq_len, dtype=jnp.float32):
            inv_freq = 1.0 / ROPE_BASE ** (jnp.arange(0, HEAD_DIM, 2, dtype=jnp.float32) / HEAD_DIM)
            pos = jnp.arange(seq_len, dtype=jnp.float32)
            freqs = jnp.outer(pos, inv_freq)
            emb = jnp.concatenate([freqs, freqs], -1)
            return (jnp.cos(emb)[None, None].astype(dtype), jnp.sin(emb)[None, None].astype(dtype))

        def block_mask(seq_len):
            i = jnp.arange(seq_len)[:, None]
            j = jnp.arange(seq_len)[None, :]
            blk = i // BLOCK == j // BLOCK
            glob = (i < N_GLOBAL) | (j < N_GLOBAL)
            slide = jnp.abs(i - j) <= WINDOW
            return (blk | glob | slide) & (j <= i)
        B, S, E = x.shape
        scale = HEAD_DIM ** (-0.5)
        qkv = x @ qkv_w.T
        qkv = qkv.reshape(B, S, 3, HEADS, HEAD_DIM)
        qkv = jnp.transpose(qkv, (2, 0, 3, 1, 4))
        q, k, v = (qkv[0], qkv[1], qkv[2])
        cos, sin = rope_cos_sin(S, x.dtype)
        q = q * cos + rotate_half(q) * sin
        k = k * cos + rotate_half(k) * sin
        mask = block_mask(S)
        scores = jnp.einsum('bhqd,bhkd->bhqk', q, k) * scale
        scores = jnp.where(mask[None, None], scores, jnp.finfo(scores.dtype).min)
        attn = jax.nn.softmax(scores, axis=-1)
        out = jnp.einsum('bhqk,bhkd->bhqd', attn, v)
        out = jnp.transpose(out, (0, 2, 1, 3)).reshape(B, S, E)
        return out @ out_w.T

    def _L0_ffn_ref(x, w1_w, w1_s, w2_w, w2_s, h1_w, h1_s, h2_w, h2_s, w3_w, w3_s):
        import jax, jax.numpy as jnp
        import numpy as np
        D_IN, D_HID = (256, 1024)

        def _ternary(key, shape):
            return jax.random.randint(key, shape, -1, 2).astype(jnp.float32)

        def _tlin(x, w, s):
            return jnp.einsum('bsi,oi->bso', x, w) * s
        h = jax.nn.silu(_tlin(x, w1_w, w1_s)) * _tlin(x, w2_w, w2_s)
        h = jax.nn.gelu(_tlin(h, h1_w, h1_s), approximate=False)
        h = jax.nn.gelu(_tlin(h, h2_w, h2_s), approximate=False)
        return _tlin(h, w3_w, w3_s)
    x = L0_attn_x
    x = x + _L0_attn_ref(_layernorm(x, axis=-1), L0_attn_qkv_w, L0_attn_out_w)
    x = x + _L0_ffn_ref(_layernorm(x, axis=-1), L0_ffn_w1_w, L0_ffn_w1_s, L0_ffn_w2_w, L0_ffn_w2_s, L0_ffn_h1_w, L0_ffn_h1_s, L0_ffn_h2_w, L0_ffn_h2_s, L0_ffn_w3_w, L0_ffn_w3_s)
    return x

_drawn_inputs = setup_inputs


def setup_inputs(seed=0):
    import zlib

    import numpy as np

    out = dict(_drawn_inputs(seed))
    spreads = {}
    factors = {}
    for name, (base, spread) in spreads.items():
        noise = np.random.default_rng([zlib.crc32(name.encode()), seed]).standard_normal(out[name].shape)
        drawn = base * np.exp(spread * noise) if base else spread * noise
        out[name] = jnp.asarray(drawn.astype(out[name].dtype))
    for name, factor in factors.items():
        out[name] = (out[name] * factor).astype(out[name].dtype)
    return out
```

```python
import concourse.bass as bass
from concourse import mybir
from contextlib import ExitStack

F32 = mybir.dt.float32
F32R = mybir.dt.float32r
U16 = mybir.dt.uint16
I32 = mybir.dt.int32
ALU = mybir.AluOpType
ACT = mybir.ActivationFunctionType
AX = mybir.AxisListType

P = 128
NB, SEQ, EMB = 8, 512, 256
HEADS, HD = 16, 16
HID = 1024
NT = SEQ // P
NF = EMB // P
NH = HID // P
HPT = P // HD
NGLOB = 4
SCALE = HD ** -0.5
LN_EPS = 1e-5
NEG = -3.0e38

UH = 4
UNITS = NT * HEADS // UH
GROUPS = HEADS // UH
LATER = UNITS - GROUPS
KEYS = 2 * P
COLS = KEYS + NGLOB
SM_RING = 3
STAT_RING = 4

T_LAG, PV_LAG = 2, 3
PVE_LAG, O_LAG, X2_LAG, LT_LAG, X2LO_LAG = 7, 8, 9, 10, 11
STEPS = UNITS + 8

W_UP, W_H1 = 0, 2 * NF * HID
W_H2 = W_H1 + NH * HID
W_DN = W_H2 + NH * HID
W_COLS = W_DN + NH * EMB
W_PARTS = [(W_UP, W_H1), (W_H1, W_H2), (W_H2, W_DN), (W_DN, W_COLS)]
CHECK = 2048
CHECKS = W_COLS // CHECK

FFN_TILES = 3 * NH
DEEP = 2 * NH
HALVES = 2 * UNITS
B6_USES = 3 + 2 * NT


def layer_kernel(nc, x, qkvT, outT, ffn_w, ffn_s, s3row, rope, mask, small, out):
    x_v = x.rearrange("b (t p) e -> b p t e", p=P)
    out_v = out.rearrange("b (t p) e -> b t p e", p=P)
    w_scratch = nc.dram_tensor("w_scratch", (P, W_COLS), F32, kind="Internal").ap()

    ctx = ExitStack()
    with ctx:
        def sem(name):
            return ctx.enter_context(nc.semaphore(name))

        base = (nc.sbuf_base + 31) // 32 * 32
        arena_bytes = (nc.sbuf_usable_end - base) // 32 * 32 - 64
        ctx.enter_context(nc.sbuf_tensor("arena", [P, arena_bytes // 4], F32))
        used = [base]

        def sb(name, shape, dt=F32, at=None):
            size = 4
            for n in shape[1:]:
                size *= n
            if at is None:
                at = used[0]
                used[0] = (at + size + 31) // 32 * 32
                assert used[0] <= base + arena_bytes, (name, used[0] - base, arena_bytes)
            return nc.alloc_sbuf_tensor_at(name, shape, dt, offset=at)

        W = sb("W", [P, W_COLS], F32R)
        a_at = used[0]
        a_hi = sb("a_hi", [P, NH, SEQ], F32R)
        a_lo = sb("a_lo", [P, NH, SEQ], F32R)
        b_at = used[0]
        b_hi = sb("b_hi", [P, NH, SEQ], F32R)
        b_lo = sb("b_lo", [P, NH, SEQ], F32R)
        Sm = sb("Sm", [P, SM_RING, UH, COLS], at=a_at)
        pt_at = a_at + SM_RING * UH * COLS * 4
        PT = sb("PT", [P, 2, 2, UH, P], at=pt_at)
        pg_at = pt_at + 2 * 2 * UH * P * 4
        PgT = sb("PgT", [UH * NGLOB, 2, P], at=pg_at)
        junk = sb("junk", [P, CHECK], at=pg_at + 2 * P * 4)
        assert pg_at + 2 * P * 4 + CHECK * 4 <= b_at
        Kz = sb("Kz", [P, HEADS, SEQ], at=b_at)
        x2_hi = sb("x2_hi", [P, NF, SEQ], F32R)
        x2_lo = sb("x2_lo", [P, NF, SEQ], F32R)
        x_in = sb("x_in", [P, NT, EMB])
        x_res = sb("x_res", [P, NT, EMB])
        featT = sb("featT", [P, NF, SEQ])
        q = sb("q", [P, NF, SEQ])
        k = sb("k", [P, NF, SEQ])
        v = sb("v", [P, NT, EMB])
        xn = sb("xn", [P, NT, EMB])
        rot = xn[:, :, :].rearrange("p (r t) e -> p r (t e)", r=2)
        silu = rot
        Vg = sb("Vg", [UH * NGLOB, EMB])
        Kg = sb("Kg", [P, NF, HPT, NGLOB])
        Pg = sb("Pg", [P, SM_RING, UH * NGLOB])
        Gs = sb("Gs", [P, HEADS, NGLOB])
        gmax = sb("gmax", [P, HEADS])
        mx = sb("mx", [P, STAT_RING, UH])
        negm = sb("negm", [P, STAT_RING, UH])
        rowsum = sb("rowsum", [P, STAT_RING, UH])
        rinv = sb("rinv", [P, STAT_RING, UH])
        bn1 = sb("bn1", [P, NT, 6])
        mv1 = sb("mv1", [P, NT, 2])
        ve1 = sb("ve1", [P, NT])
        rstd1 = sb("rstd1", [P, NT])
        bn2 = sb("bn2", [P, NT, 6])
        mv2 = sb("mv2", [P, NT, 2])
        ve2 = sb("ve2", [P, NT])
        rstd2 = sb("rstd2", [P, NT])
        low_sum = sb("low_sum", [P, CHECKS])
        low_all = sb("low_all", [P, 1])
        low_row = sb("low_row", [1, P])
        low_max = sb("low_max", [1, 1])
        low_int = sb("low_int", [1, 1], I32)
        qkv_w = sb("qkv_w", [P, NF, 3 * EMB])
        out_w = sb("out_w", [P, NF, EMB])
        scales = sb("scales", [P, 4, NH])
        s3 = sb("s3", [P, EMB])
        cos_sin = sb("cos_sin", [P, 2, SEQ])
        msk = sb("msk", [P, KEYS])
        consts = sb("consts", [P, small.shape[1]])
        at = 0
        ident = consts[:, at:at + P]
        at += P
        headmask = consts[:, at:at + HPT]
        at += HPT
        headmask4 = consts[:, at:at + HPT * NGLOB].rearrange("p (h j) -> p h j", j=NGLOB)
        at += HPT * NGLOB
        gmask = consts[:, at:at + 3 * NGLOB].rearrange("p (i j) -> p i j", j=NGLOB)
        at += 3 * NGLOB
        even_odd = consts[:, at:at + 2]
        at += 2
        minus_half = consts[:, at:at + 1]
        at += 1
        pick_glob = consts[:, at:at + UH * NGLOB]
        at += UH * NGLOB
        vg_mask = consts[0:UH * NGLOB, at:at + EMB]
        at += EMB
        assert at == small.shape[1]

        bank = [ctx.enter_context(nc.psum_tensor(f"bank{i}", [P, 512], F32)) for i in range(8)]

        attn_loaded = sem("attn_loaded")
        scratch_written = [sem(f"scratch_written{n}") for n in range(len(W_PARTS))]
        w_loaded = [sem(f"w_loaded{n}") for n in range(len(W_PARTS))]
        x_loaded = sem("x_loaded")
        y_stored = sem("y_stored")
        low_moved = sem("low_moved")
        low_summed = sem("low_summed")
        low_found = sem("low_found")
        low_ready = sem("low_ready")
        bn1_done = sem("bn1_done")
        mv1_done = sem("mv1_done")
        ve1_done = sem("ve1_done")
        rstd1_done = sem("rstd1_done")
        xn1_done = sem("xn1_done")
        ln1_turned = sem("ln1_turned")
        xnT_done = sem("xnT_done")
        qk_done = sem("qk_done")
        rot_done = sem("rot_done")
        cos_done = sem("cos_done")
        sin_done = sem("sin_done")
        rope_done = sem("rope_done")
        v_done = sem("v_done")
        v_kept = sem("v_kept")
        vg_done = sem("vg_done")
        vg_kept = sem("vg_kept")
        down_done = sem("down_done")
        down_scaled = sem("down_scaled")
        y_done = sem("y_done")
        kz_low = sem("kz_low")
        kz_high = sem("kz_high")
        kg_done = sem("kg_done")
        g_done = sem("g_done")
        gs_done = sem("gs_done")
        b6_free = sem("b6_free")
        s_done = sem("s_done")
        s_free = sem("s_free")
        negm_done = sem("negm_done")
        exp_done = sem("exp_done")
        rinv_done = sem("rinv_done")
        norm_done = sem("norm_done")
        pg_done = sem("pg_done")
        cur_turned = sem("cur_turned")
        prev_turned = sem("prev_turned")
        glob_turned = sem("glob_turned")
        cur_kept = sem("cur_kept")
        prev_kept = sem("prev_kept")
        glob_kept = sem("glob_kept")
        pv_done = sem("pv_done")
        pv_even_kept = sem("pv_even_kept")
        pv_kept = sem("pv_kept")
        o_done = sem("o_done")
        x1_done = sem("x1_done")
        bn2_done = sem("bn2_done")
        mv2_done = sem("mv2_done")
        ve2_done = sem("ve2_done")
        rstd2_done = sem("rstd2_done")
        xn2_done = sem("xn2_done")
        ln2_turned = sem("ln2_turned")
        x2hi_done = sem("x2hi_done")
        x2lo_done = sem("x2lo_done")
        gate_done = sem("gate_done")
        up_done = sem("up_done")
        silu_done = sem("silu_done")
        mul_done = sem("mul_done")
        uphi_done = sem("uphi_done")
        deep_done = sem("deep_done")
        gelu_done = sem("gelu_done")
        ffn_free = sem("ffn_free")

        def at_round(b, per, n):
            return b * per + n

        block = ctx.enter_context(nc.Block())

        N_CONST = 8

        @block.sync
        def _(sp):
            def load_x(b):
                sp.dma_start(x_in[:, :, :], x_v[b]).then_inc(x_loaded, 16)

            def store_y(b):
                for t in range(NT):
                    sp.wait_ge(y_done, at_round(b, NT, t + 1))
                    sp.dma_start(out_v[b, t], x_res[:, t, :]).then_inc(y_stored, 16)

            def next_x(b):
                sp.wait_ge(x1_done, at_round(b, NT, NT))
                load_x(b + 1)

            load_x(0)
            sp.dma_start(consts[:, :], small).then_inc(attn_loaded, 16)
            sp.dma_start(qkv_w[:, :, :], qkvT).then_inc(attn_loaded, 16)
            sp.dma_start(cos_sin[:, :, :], rope).then_inc(attn_loaded, 16)
            sp.dma_start(msk[:, :], mask).then_inc(attn_loaded, 16)
            sp.dma_start(out_w[:, :, :], outT).then_inc(attn_loaded, 16)
            sp.dma_start(scales[:, :, :], ffn_s).then_inc(attn_loaded, 16)
            sp.dma_start(s3[:, :], s3row.broadcast_to([P, EMB])).then_inc(attn_loaded, 16)
            for n, (c0, c1) in enumerate(W_PARTS):
                sp.dma_start(w_scratch[:, c0:c1], ffn_w[:, c0:c1]).then_inc(scratch_written[n], 16)
            for n, (c0, c1) in enumerate(W_PARTS):
                sp.wait_ge(scratch_written[n], 16)
                sp.dma_start(W[:, c0:c1].bitcast(F32), w_scratch[:, c0:c1]).then_inc(w_loaded[n], 16)
            sp.wait_ge(low_found, 1)
            sp.dma_start(low_row[0:1, :].rearrange("a (p o) -> a p o", o=1), low_all[:, :])\
                .then_inc(low_moved, 16)

            next_x(0)
            with sp.Fori(1, NB - 1) as b:
                store_y(b - 1)
                next_x(b)
            store_y(NB - 2)
            store_y(NB - 1)
            sp.wait_ge(y_stored, 16 * NT * NB)

        @block.tensor
        def _(pe):
            def ln1_transposes(b):
                for t in range(NT):
                    pe.wait_ge(xn1_done, at_round(b, NT, t + 1))
                    for f in range(NF):
                        mm = nc.tensor.transpose(bank[4 + f][:, t * P:(t + 1) * P],
                                                 xn[:, t, f * P:(f + 1) * P], ident)
                        if t == NT - 1:
                            mm.then_inc(ln1_turned, 1)

            def qk_projection(b):
                pe.wait_ge(xnT_done, at_round(b, NF, NF))
                for n in range(2 * NF):
                    f, kind = n // 2, n % 2
                    col = kind * EMB + f * P
                    for kk in range(NF):
                        mm = nc.tensor.matmul(bank[[6, 7, 4, 5][n]][:, :], qkv_w[:, kk, col:col + P],
                                              featT[:, kk, :], start=(kk == 0), stop=(kk == NF - 1))
                    mm.then_inc(qk_done, 1)

            def v_projection(b):
                for t in range(NT):
                    pe.wait_ge(rot_done, at_round(b, 2 * NF, t + 1))
                    for kk in range(NF):
                        mm = nc.tensor.matmul(bank[[6, 7, 4, 5][t]][:, 0:EMB], featT[:, kk, t * P:(t + 1) * P],
                                              qkv_w[:, kk, 2 * EMB:3 * EMB], start=(kk == 0), stop=(kk == NF - 1))
                    mm.then_inc(v_done, 1)
                pe.wait_ge(v_kept, at_round(b, NT, 1))
                nc.tensor.matmul(bank[6][0:UH * NGLOB, 0:EMB], pick_glob, v[:, 0, :],
                                 start=True, stop=True).then_inc(vg_done, 1)

            def ffn_down(b, nxt, general):
                pe.wait_ge(ffn_free, at_round(b, FFN_TILES, FFN_TILES))
                for t in range(NT):
                    if nxt is not None:
                        if t < NT - 1:
                            pe.wait_ge(v_kept, at_round(nxt, NT, t + 2))
                        else:
                            pe.wait_ge(vg_kept, at_round(nxt, 1, 1))
                    for kk in range(NH):
                        for part, h in enumerate((a_hi, a_lo)):
                            lhsT = h[:, kk, t * P:(t + 1) * P]
                            rhs = W[:, W_DN + kk * EMB:W_DN + (kk + 1) * EMB]
                            if general:
                                lhsT, rhs = lhsT.bitcast(F32), rhs.bitcast(F32)
                            mm = nc.tensor.matmul(bank[[7, 4, 5, 6][t]][:, 0:EMB], lhsT, rhs,
                                                  start=(kk == 0 and part == 0), stop=(kk == NH - 1 and part == 1))
                    mm.then_inc(down_done, 1)

            def attention(b, first):
                b6 = [0]

                def next_b6():
                    if b6[0]:
                        pe.wait_ge(b6_free, at_round(b, B6_USES, b6[0]))
                    b6[0] += 1

                def global_scores(i):
                    next_b6()
                    if i == 1:
                        pe.wait_ge(kg_done, at_round(b, 1, 1))
                    for f in range(NF):
                        mm = nc.tensor.matmul(bank[6][:, f * HPT * NGLOB:(f + 1) * HPT * NGLOB],
                                              q[:, f, i * P:(i + 1) * P],
                                              Kg[:, f, :, :].rearrange("p h j -> p (h j)"), start=True, stop=True)
                    mm.then_inc(g_done, 1)

                def scores(n):
                    i, g = n // GROUPS, n % GROUPS
                    if i == 0:
                        f = g * UH // HPT
                        pe.wait_ge(rope_done, at_round(b, 2 * NF, 2 * f + 1))
                        if f == 0:
                            pe.wait_ge(kz_low, at_round(b, HPT, UH * (g + 1)))
                        else:
                            pe.wait_ge(kz_high, at_round(b, HPT, UH * (g + 1) - HPT))
                    lo = 0 if i else P
                    for half in range(2):
                        hs = 2 * n + half
                        if hs >= 3:
                            pe.wait_ge(s_free, at_round(b, HALVES, hs - 2))
                        for c2 in range(2):
                            h = g * UH + 2 * half + c2
                            mm = nc.tensor.matmul(bank[hs % 3][:, c2 * KEYS + lo:(c2 + 1) * KEYS],
                                                  q[:, h // HPT, i * P:(i + 1) * P],
                                                  Kz[:, h, i * P + lo - P:(i + 1) * P], start=True, stop=True)
                        mm.then_inc(s_done, 1)

                def transposes(n):
                    i = n // GROUPS
                    pe.wait_ge(norm_done, at_round(b, UNITS, n + 1))
                    if n:
                        pe.wait_ge(cur_kept, at_round(b, UNITS, n))
                    for c in range(UH):
                        mm = nc.tensor.transpose(bank[5][:, c * P:(c + 1) * P], Sm[:, n % SM_RING, c, P:KEYS], ident)
                    mm.then_inc(cur_turned, 1)
                    if i == 0:
                        return
                    m = n - GROUPS
                    if m:
                        pe.wait_ge(prev_kept, at_round(b, LATER, m))
                        pe.wait_ge(glob_kept, at_round(b, LATER, m))
                    for c in range(UH):
                        mm = nc.tensor.transpose(bank[4][:, c * P:(c + 1) * P], Sm[:, n % SM_RING, c, 0:P], ident)
                    mm.then_inc(prev_turned, 1)
                    pe.wait_ge(pg_done, at_round(b, LATER, m + 1))
                    nc.tensor.transpose(bank[3][0:UH * NGLOB, 0:P], Pg[:, n % SM_RING, :], ident)\
                        .then_inc(glob_turned, 1)

                def weighted_values(n):
                    i, g = n // GROUPS, n % GROUPS
                    f = g * UH // HPT
                    pe.wait_ge(cur_kept, at_round(b, UNITS, n + 1))
                    if i:
                        pe.wait_ge(prev_kept, at_round(b, LATER, n - GROUPS + 1))
                        pe.wait_ge(glob_kept, at_round(b, LATER, n - GROUPS + 1))
                        if g == 0:
                            pe.wait_ge(pv_kept, at_round(b, NT, i))
                    for side in ((1, 0) if i else (1,)):
                        for c in range(UH):
                            col = f * P + 32 * c
                            mm = nc.tensor.matmul(bank[7][32 * c:32 * c + 32, g * P:(g + 1) * P],
                                                  v[:, i - 1 + side, col:col + 32], PT[:, n % 2, side, c, :],
                                                  start=(side == 1), stop=(i == 0), skip_group_check=True)
                    if i:
                        mm = nc.tensor.matmul(bank[7][:, g * P:(g + 1) * P], Vg[:, f * P:(f + 1) * P],
                                              PgT[:, n % 2, :], start=False, stop=True, skip_group_check=True)
                    mm.then_inc(pv_done, 1)

                def out_projection(i):
                    next_b6()
                    pe.wait_ge(pv_kept, at_round(b, NT, i + 1))
                    for f in range(NF):
                        mm = nc.tensor.matmul(bank[6][:, 0:EMB], featT[:, f, i * P:(i + 1) * P], out_w[:, f, :],
                                              start=(f == 0), stop=(f == NF - 1))
                    mm.then_inc(o_done, 1)

                def ln2_transposes(i):
                    next_b6()
                    pe.wait_ge(xn2_done, at_round(b, NT, i + 1))
                    for f in range(NF):
                        mm = nc.tensor.transpose(bank[6][:, f * P:(f + 1) * P], xn[:, i, f * P:(f + 1) * P], ident)
                    mm.then_inc(ln2_turned, 1)

                pe.wait_ge(v_kept, at_round(b, NT, NT))
                pe.wait_ge(vg_kept, at_round(b, 1, 1))
                if not first:
                    pe.wait_ge(ffn_free, at_round(b, FFN_TILES, 0))
                    pe.wait_ge(y_done, at_round(b, NT, 0))
                for n in range(STEPS):
                    if n < UNITS:
                        if n >= GROUPS and n % GROUPS == 0:
                            global_scores(n // GROUPS)
                        scores(n)
                    if 0 <= n - T_LAG < UNITS:
                        transposes(n - T_LAG)
                    if 0 <= n - PV_LAG < UNITS:
                        weighted_values(n - PV_LAG)
                    if n >= O_LAG and (n - O_LAG) % GROUPS == 0 and (n - O_LAG) // GROUPS < NT:
                        out_projection((n - O_LAG) // GROUPS)
                    if n >= LT_LAG and (n - LT_LAG) % GROUPS == 0 and (n - LT_LAG) // GROUPS < NT:
                        ln2_transposes((n - LT_LAG) // GROUPS)

            def ffn_tile(out, w_at, width, m, h_hi, h_lo, tiles, general, wait=None):
                for kk in range(tiles):
                    if wait is not None:
                        wait(kk)
                    lhsT = W[:, w_at + kk * width + m * P:w_at + kk * width + (m + 1) * P]
                    if general:
                        lhsT = lhsT.bitcast(F32)
                    for part, h in enumerate((h_hi, h_lo)):
                        rhs = h[:, kk, :].bitcast(F32) if general else h[:, kk, :]
                        mm = nc.tensor.matmul(out, lhsT, rhs, start=(kk == 0 and part == 0),
                                              stop=(kk == tiles - 1 and part == 1))
                return mm

            def ffn_hidden(b, general):
                pe.wait_ge(x2hi_done, at_round(b, NT, NT))
                pe.wait_ge(x2lo_done, at_round(b, NT, NT))
                pe.wait_ge(s_free, at_round(b, HALVES, HALVES))
                pe.wait_ge(glob_kept, at_round(b, LATER, LATER))
                for m in range(NH):
                    if m >= 2:
                        pe.wait_ge(ffn_free, at_round(b, FFN_TILES, m - 1))
                    pair = 2 * (m % 2)
                    ffn_tile(bank[pair][:, :], W_UP, HID, m, x2_hi, x2_lo, NF, general).then_inc(gate_done, 1)
                    ffn_tile(bank[pair + 1][:, :], W_UP + NF * HID, HID, m, x2_hi, x2_lo, NF, general)\
                        .then_inc(up_done, 1)
                for layer, (w_at, h_hi, h_lo) in enumerate(((W_H1, a_hi, a_lo), (W_H2, b_hi, b_lo))):
                    for m in range(NH):
                        before = NH * (layer + 1)
                        pe.wait_ge(ffn_free, at_round(b, FFN_TILES, before + m - 3 if layer or m >= 4 else
                                                      before - 1 + m // 2 if m < 2 else before))
                        wait = None
                        if m == 0:
                            def wait(kk, before=before):
                                if kk >= NH - 4:
                                    pe.wait_ge(ffn_free, at_round(b, FFN_TILES, before - NH + kk + 1))
                        ffn_tile(bank[m % 4][:, :], w_at, HID, m, h_hi, h_lo, NH, general, wait)\
                            .then_inc(deep_done, 1)

            pe.wait_ge(attn_loaded, 16 * (N_CONST - 1))
            ln1_transposes(0)
            qk_projection(0)
            v_projection(0)
            attention(0, True)
            pe.wait_ge(low_ready, 1)
            low_bits = pe.value_load(low_int[0:1, 0:1], min_val=0, max_val=1)

            def rounds(general):
                ffn_hidden(0, general)
                with pe.Fori(1, NB) as b:
                    ln1_transposes(b)
                    qk_projection(b)
                    v_projection(b)
                    ffn_down(b - 1, b, general)
                    attention(b, False)
                    ffn_hidden(b, general)
                ffn_down(NB - 1, None, general)

            with pe.If(low_bits):
                rounds(True)
            with pe.Else():
                rounds(False)

        @block.scalar
        def _(act):
            def before_attention(b):
                for f in range(NF):
                    act.wait_ge(ln1_turned, at_round(b, NF, f + 1))
                    nc.scalar.copy(featT[:, f, :], bank[4 + f][:, :]).then_inc(xnT_done, 1)
                for t in range(NT):
                    act.wait_ge(v_done, at_round(b, NT, t + 1))
                    nc.scalar.copy(v[:, t, :], bank[[6, 7, 4, 5][t]][:, 0:EMB]).then_inc(v_kept, 1)

            def attention(b, first):
                def exponentials(n):
                    i, r = n // GROUPS, n % STAT_RING
                    c0, c1 = (0, COLS) if i else (P, KEYS)
                    act.wait_ge(negm_done, at_round(b, UNITS, n + 1))
                    for c in range(UH):
                        row = Sm[:, n % SM_RING, c, c0:c1]
                        ex = nc.scalar.activation(row, row, ACT.Exp, bias=negm[:, r, c:c + 1], scale=SCALE,
                                                  accum_out=rowsum[:, r, c:c + 1])
                    ex.then_inc(exp_done, 1)

                def keep_prev(n):
                    act.wait_ge(prev_turned, at_round(b, LATER, n - GROUPS + 1))
                    act.wait_ge(pv_done, at_round(b, UNITS, n - 1))
                    nc.scalar.copy(PT[:, n % 2, 0, :, :].rearrange("p c q -> p (c q)"), bank[4][:, :])\
                        .then_inc(prev_kept, 1)

                def keep_even_heads(i):
                    act.wait_ge(pv_done, at_round(b, UNITS, GROUPS * (i + 1)))
                    nc.scalar.activation(featT[:, :, i * P:(i + 1) * P],
                                         bank[7][:, :].rearrange("p (f s q) -> p f s q", f=NF, s=2)[:, :, 0, :],
                                         ACT.Copy, scale=even_odd[:, 0:1]).then_inc(pv_even_kept, 1)

                def keep_x2hi(i):
                    act.wait_ge(ln2_turned, at_round(b, NT, i + 1))
                    nc.scalar.copy(x2_hi[:, :, i * P:(i + 1) * P],
                                   bank[6][:, 0:EMB].rearrange("p (f q) -> p f q", f=NF)).then_inc(x2hi_done, 1)

                for n in range(STEPS):
                    if n < UNITS:
                        exponentials(n)
                    if GROUPS <= n - T_LAG < UNITS:
                        keep_prev(n - T_LAG)
                    if n >= PVE_LAG and (n - PVE_LAG) % GROUPS == 0 and (n - PVE_LAG) // GROUPS < NT:
                        keep_even_heads((n - PVE_LAG) // GROUPS)
                    if n >= LT_LAG and (n - LT_LAG) % GROUPS == 0 and (n - LT_LAG) // GROUPS < NT:
                        keep_x2hi((n - LT_LAG) // GROUPS)
                    if first and n >= STEPS - CHECKS:
                        check_weights(n - (STEPS - CHECKS))

            def check_weights(n):
                c1 = (n + 1) * CHECK
                part = [c1 <= end for _, end in W_PARTS].index(True)
                act.wait_ge(w_loaded[part], 16)
                if n:
                    act.wait_ge(low_summed, n)
                nc.scalar.activation(junk[:, :], W[:, c1 - CHECK:c1].bitcast(U16)[:, 0:2 * CHECK:2], ACT.Copy,
                                     accum_out=low_sum[:, n:n + 1]).then_inc(low_summed, 1)

            def ffn_hidden(b):
                def keep_up_hi(m):
                    act.wait_ge(mul_done, at_round(b, NH, m + 1))
                    nc.scalar.copy(a_hi[:, m, :], bank[2 * (m % 2) + 1][:, :]).then_inc(uphi_done, 1)

                for m in range(NH):
                    act.wait_ge(gate_done, at_round(b, NH, m + 1))
                    if m >= 2:
                        act.wait_ge(mul_done, at_round(b, NH, m - 1))
                    nc.scalar.activation(silu[:, m % 2, :], bank[2 * (m % 2)][:, :], ACT.Silu,
                                         scale=scales[:, 0, m:m + 1]).then_inc(silu_done, 1)
                    if m:
                        keep_up_hi(m - 1)
                keep_up_hi(NH - 1)
                for n in range(DEEP):
                    layer, m = n // NH, n % NH
                    h_hi = (b_hi, a_hi)[layer]
                    ps = bank[m % 4][:, :]
                    s = scales[:, 2 + layer, m:m + 1]
                    act.wait_ge(deep_done, at_round(b, DEEP, n + 1))
                    nc.scalar.activation(h_hi[:, m, :], ps, ACT.Gelu, scale=s)
                    nc.scalar.activation(ps, ps, ACT.Gelu, scale=s).then_inc(gelu_done, 1)

            act.wait_ge(attn_loaded, 16 * (N_CONST - 1))
            before_attention(0)
            attention(0, True)
            ffn_hidden(0)
            with act.Fori(1, NB) as b:
                before_attention(b)
                attention(b, False)
                ffn_hidden(b)

        @block.vector
        def _(dve):
            def ln1_stats(b, t):
                if t == 0:
                    dve.wait_ge(x_loaded, at_round(b, 16, 16))
                nc.vector.bn_stats(bn1[:, t, :], x_in[:, t, :]).then_inc(bn1_done, 1)
                dve.wait_ge(bn1_done, at_round(b, NT, t + 1))
                dve.nop(nofuse=True)
                nc.vector.bn_aggr(mv1[:, t, :], bn1[:, t, :]).then_inc(mv1_done, 1)

            def ln1_apply(b, t):
                dve.wait_ge(rstd1_done, at_round(b, NT, t + 1))
                nc.vector.tensor_scalar(xn[:, t, :], x_in[:, t, :], mv1[:, t, 0:1], rstd1[:, t:t + 1],
                                        ALU.subtract, ALU.mult).then_inc(xn1_done, 1)

            def rope(b):
                for n in range(2 * NF):
                    src = bank[[6, 7, 4, 5][n]]
                    dst = (q, k)[n % 2][:, n // 2, :]
                    dve.wait_ge(qk_done, at_round(b, 2 * NF, n + 1))
                    if n >= 2:
                        dve.wait_ge(rope_done, at_round(b, 2 * NF, n - 1))
                    nc.vector.tensor_tensor(dst, src[:, :], cos_sin[:, 0, :], ALU.mult).then_inc(cos_done, 1)
                    nc.vector.stream_shuffle(rot[:, n % 2, :], src[:, :], [p ^ 1 for p in range(32)])\
                        .then_inc(rot_done, 1)

            def keep_vg(b):
                dve.wait_ge(vg_done, at_round(b, 1, 1))
                nc.vector.tensor_tensor(Vg[:, :], bank[6][0:UH * NGLOB, 0:EMB], vg_mask, ALU.mult)\
                    .then_inc(vg_kept, 1)

            def pad_keys(b, h0, first):
                if h0 == 0:
                    dve.wait_ge(rope_done, at_round(b, 2 * NF, 2))
                    if not first:
                        dve.wait_ge(deep_done, at_round(b, DEEP, 0))
                for h in range(h0, h0 + UH):
                    nc.vector.tensor_scalar(Kz[:, h, :], k[:, 0, :], headmask[:, h:h + 1], None, ALU.mult)\
                        .then_inc(kz_low, 1)

            def global_keys(b):
                dve.wait_ge(rope_done, at_round(b, 2 * NF, 2 * NF))
                nc.vector.tensor_tensor(
                    Kg[:, :, :, :], k[:, :, 0:NGLOB].unsqueeze(2).broadcast_to([P, NF, HPT, NGLOB]),
                    headmask4.unsqueeze(1).broadcast_to([P, NF, HPT, NGLOB]), ALU.mult).then_inc(kg_done, 1)

            def finish_y(b):
                for t in range(NT):
                    ps = bank[[7, 4, 5, 6][t]][:, 0:EMB]
                    dve.wait_ge(down_done, at_round(b, NT, t + 1))
                    nc.vector.tensor_tensor(ps, ps, s3[:, :], ALU.mult).then_inc(down_scaled, 1)
                    dve.wait_ge(down_scaled, at_round(b, NT, t + 1))
                    nc.vector.tensor_tensor(x_res[:, t, :], x_res[:, t, :], ps, ALU.add).then_inc(y_done, 1)

            def attention(b, first):
                def global_scores(i):
                    dve.wait_ge(g_done, at_round(b, NT - 1, i))
                    nc.vector.tensor_tensor(
                        Gs[:, :, :], bank[6][:, 0:HEADS * NGLOB].rearrange("p (h j) -> p h j", j=NGLOB),
                        gmask[:, i - 1:i, :].broadcast_to([P, HEADS, NGLOB]), ALU.add).then_inc(b6_free, 1)
                    dve.wait_ge(b6_free, at_round(b, B6_USES, (1, 2, 5)[i - 1]))
                    nc.vector.tensor_reduce(gmax[:, :], Gs[:, :, :], AX.X, ALU.max).then_inc(gs_done, 1)
                    dve.wait_ge(gs_done, at_round(b, NT - 1, i))

                def masked_max(n):
                    i, g, r = n // GROUPS, n % GROUPS, n % STAT_RING
                    lo = 0 if i else P
                    buf = Sm[:, n % SM_RING, :, :]
                    if n >= SM_RING:
                        m = n - SM_RING
                        if m < GROUPS:
                            dve.wait_ge(cur_turned, at_round(b, UNITS, m + 1))
                        else:
                            dve.wait_ge(glob_turned, at_round(b, LATER, m - GROUPS + 1))
                    if i:
                        nc.vector.tensor_copy(buf[:, :, KEYS:COLS], Gs[:, g * UH:(g + 1) * UH, :])
                    for half in range(2):
                        hs = 2 * n + half
                        dve.wait_ge(s_done, at_round(b, HALVES, hs + 1))
                        dve.nop(nofuse=True)
                        for c2 in range(2):
                            c = 2 * half + c2
                            h = g * UH + c
                            tt = nc.vector.tensor_tensor_reduce(
                                out=buf[:, c, lo:KEYS], in0=bank[hs % 3][:, c2 * KEYS + lo:(c2 + 1) * KEYS],
                                in1=msk[:, lo:KEYS], scale=1.0, scalar=gmax[:, h:h + 1] if i else NEG,
                                op0=ALU.add, op1=ALU.max, accum_out=mx[:, r, c:c + 1])
                        tt.then_inc(s_free, 1)
                    dve.wait_ge(s_free, at_round(b, HALVES, 2 * n + 2))
                    nc.vector.tensor_scalar(negm[:, r, :], mx[:, r, :], -SCALE, None, ALU.mult).then_inc(negm_done, 1)

                def inverse_sums(n):
                    r = n % STAT_RING
                    dve.wait_ge(exp_done, at_round(b, UNITS, n + 1))
                    nc.vector.reciprocal(rinv[:, r, :], rowsum[:, r, :]).then_inc(rinv_done, 1)

                def keep_cur(n):
                    dve.wait_ge(cur_turned, at_round(b, UNITS, n + 1))
                    if n >= 2:
                        dve.wait_ge(pv_done, at_round(b, UNITS, n - 1))
                    nc.vector.tensor_copy(PT[:, n % 2, 1, :, :].rearrange("p c q -> p (c q)"), bank[5][:, :])\
                        .then_inc(cur_kept, 1)
                    if n >= GROUPS:
                        dve.wait_ge(glob_turned, at_round(b, LATER, n - GROUPS + 1))
                        nc.vector.tensor_copy(PgT[:, n % 2, :], bank[3][0:UH * NGLOB, 0:P]).then_inc(glob_kept, 1)

                def keep_odd_heads(i):
                    dve.wait_ge(pv_even_kept, at_round(b, NT, i + 1))
                    dst = featT[:, :, i * P:(i + 1) * P]
                    nc.vector.scalar_tensor_tensor(
                        dst, bank[7][:, :].rearrange("p (f s q) -> p f s q", f=NF, s=2)[:, :, 1, :],
                        even_odd[:, 1:2], dst, ALU.mult, ALU.add).then_inc(pv_kept, 1)

                def residual(i):
                    dve.wait_ge(o_done, at_round(b, NT, i + 1))
                    if not first and i == 0:
                        dve.wait_ge(y_stored, at_round(b, 16 * NT, 0))
                    nc.vector.tensor_tensor(x_res[:, i, :], x_in[:, i, :], bank[6][:, 0:EMB], ALU.add)\
                        .then_inc(b6_free, 1)
                    dve.wait_ge(b6_free, at_round(b, B6_USES, (3, 6, 8, 10)[i]))
                    nc.vector.bn_stats(bn2[:, i, :], x_res[:, i, :]).then_inc(x1_done, 1)
                    dve.wait_ge(x1_done, at_round(b, NT, i + 1))
                    dve.nop(nofuse=True)
                    nc.vector.bn_aggr(mv2[:, i, :], bn2[:, i, :]).then_inc(mv2_done, 1)

                def ln2_apply(i):
                    dve.wait_ge(rstd2_done, at_round(b, NT, i + 1))
                    nc.vector.tensor_scalar(xn[:, i, :], x_res[:, i, :], mv2[:, i, 0:1], rstd2[:, i:i + 1],
                                            ALU.subtract, ALU.mult).then_inc(xn2_done, 1)

                def keep_x2lo(i):
                    dve.wait_ge(x2hi_done, at_round(b, NT, i + 1))
                    nc.vector.tensor_tensor(
                        x2_lo[:, :, i * P:(i + 1) * P], bank[6][:, 0:EMB].rearrange("p (f q) -> p f q", f=NF),
                        x2_hi[:, :, i * P:(i + 1) * P].bitcast(F32), ALU.subtract).then_inc(x2lo_done, 1)
                    dve.wait_ge(x2lo_done, at_round(b, NT, i + 1))
                    dve.sem_inc(b6_free, 1)

                for n in range(STEPS):
                    if n < UNITS:
                        if n >= GROUPS and n % GROUPS == 0:
                            global_scores(n // GROUPS)
                        masked_max(n)
                    if 0 <= n - 1 < UNITS:
                        inverse_sums(n - 1)
                    if 0 <= n - T_LAG < UNITS:
                        keep_cur(n - T_LAG)
                    for lag, stage in ((PVE_LAG, keep_odd_heads), (O_LAG, residual), (X2_LAG, ln2_apply),
                                       (X2LO_LAG, keep_x2lo)):
                        if n >= lag and (n - lag) % GROUPS == 0 and (n - lag) // GROUPS < NT:
                            stage((n - lag) // GROUPS)
                    if first and n == STEPS - 1:
                        low_bits()

            def low_bits():
                dve.wait_ge(low_summed, CHECKS)
                nc.vector.tensor_reduce(low_all[:, :], low_sum[:, :], AX.X, ALU.max).then_inc(low_found, 1)
                dve.wait_ge(low_moved, 16)
                nc.vector.tensor_reduce(low_max[:, :], low_row[:, :], AX.X, ALU.max).then_inc(low_found, 1)
                dve.wait_ge(low_found, 2)
                nc.vector.tensor_scalar(low_int[:, :], low_max[:, :], 0.0, None, ALU.is_gt).then_inc(low_ready, 1)

            def ffn_hidden(b, last):
                def up_lo(m):
                    dve.wait_ge(uphi_done, at_round(b, NH, m + 1))
                    nc.vector.tensor_tensor(a_lo[:, m, :], bank[2 * (m % 2) + 1][:, :],
                                            a_hi[:, m, :].bitcast(F32), ALU.subtract).then_inc(ffn_free, 1)

                for m in range(NH):
                    ps = bank[2 * (m % 2) + 1][:, :]
                    dve.wait_ge(up_done, at_round(b, NH, m + 1))
                    dve.wait_ge(silu_done, at_round(b, NH, m + 1))
                    nc.vector.scalar_tensor_tensor(ps, ps, scales[:, 1, m:m + 1], silu[:, m % 2, :],
                                                   ALU.mult, ALU.mult).then_inc(mul_done, 1)
                    if m:
                        up_lo(m - 1)
                up_lo(NH - 1)
                for n in range(DEEP):
                    layer, m = n // NH, n % NH
                    h_hi, h_lo = ((b_hi, b_lo), (a_hi, a_lo))[layer]
                    dve.wait_ge(gelu_done, at_round(b, DEEP, n + 1))
                    nc.vector.tensor_tensor(h_lo[:, m, :], bank[m % 4][:, :], h_hi[:, m, :].bitcast(F32),
                                            ALU.subtract).then_inc(ffn_free, 1)
                    if not last:
                        if NH <= n < NH + NT:
                            ln1_stats(b + 1, n - NH)
                        if NH + 2 <= n < NH + 2 + NT:
                            ln1_apply(b + 1, n - NH - 2)

            def one_round(b, first=False, last=False):
                rope(b)
                keep_vg(b)
                pad_keys(b, 0, first)
                pad_keys(b, UH, first)
                global_keys(b)
                if not first:
                    finish_y(b - 1)
                attention(b, first)
                ffn_hidden(b, last)

            for t in range(NT):
                ln1_stats(0, t)
            for t in range(NT):
                ln1_apply(0, t)
            dve.wait_ge(attn_loaded, 16 * (N_CONST - 1))
            one_round(0, first=True)
            with dve.Fori(1, NB - 1) as b:
                one_round(b)
            one_round(NB - 1, last=True)
            finish_y(NB - 1)

        @block.gpsimd
        def _(pool):
            def rsqrt(b, t, mv, ve, rstd, stats, ve_done, done):
                pool.wait_ge(stats, at_round(b, NT, t + 1))
                pool.nop(nofuse=True)
                nc.gpsimd.tensor_scalar(ve[:, t:t + 1], mv[:, t, 1:2], LN_EPS, None, ALU.add).then_inc(ve_done, 1)
                pool.wait_ge(ve_done, at_round(b, NT, t + 1))
                nc.gpsimd.tensor_tensor(rstd[:, t:t + 1], ve[:, t:t + 1], minus_half, ALU.pow).then_inc(done, 1)

            def ln1(b):
                for t in range(NT):
                    rsqrt(b, t, mv1, ve1, rstd1, mv1_done, ve1_done, rstd1_done)

            def rope(b):
                for n in range(2 * NF):
                    dst = (q, k)[n % 2][:, n // 2, :]
                    pool.wait_ge(rot_done, at_round(b, 2 * NF, n + 1))
                    nc.gpsimd.tensor_tensor(rot[:, n % 2, :], rot[:, n % 2, :], cos_sin[:, 1, :], ALU.mult)\
                        .then_inc(sin_done, 1)
                    pool.wait_ge(sin_done, at_round(b, 2 * NF, n + 1))
                    pool.wait_ge(cos_done, at_round(b, 2 * NF, n + 1))
                    nc.gpsimd.tensor_tensor(dst, dst, rot[:, n % 2, :], ALU.add).then_inc(rope_done, 1)

            def pad_keys(b, first):
                pool.wait_ge(rope_done, at_round(b, 2 * NF, 2 * NF))
                if not first:
                    pool.wait_ge(deep_done, at_round(b, DEEP, 0))
                pool.nop(nofuse=True)
                for h in range(HPT):
                    nc.gpsimd.tensor_scalar(Kz[:, HPT + h, :], k[:, 1, :], headmask[:, h:h + 1], 1.0,
                                            ALU.mult, ALU.mult).then_inc(kz_high, 1)

            def attention(b):
                for n in range(UNITS):
                    i, r = n // GROUPS, n % STAT_RING
                    c0, c1 = (0 if i else P), KEYS
                    pool.wait_ge(rinv_done, at_round(b, UNITS, n + 1))
                    if i:
                        nc.gpsimd.tensor_tensor(
                            Pg[:, n % SM_RING, :].rearrange("p (c j) -> p c j", j=NGLOB),
                            Sm[:, n % SM_RING, :, KEYS:COLS],
                            rinv[:, r, :].unsqueeze(2).broadcast_to([P, UH, NGLOB]), ALU.mult).then_inc(pg_done, 1)
                    rows = Sm[:, n % SM_RING, :, c0:c1]
                    nc.gpsimd.tensor_tensor(rows, rows, rinv[:, r, :].unsqueeze(2).broadcast_to([P, UH, c1 - c0]),
                                            ALU.mult).then_inc(norm_done, 1)
                    if n >= O_LAG - 1 and (n - O_LAG + 1) % GROUPS == 0:
                        rsqrt(b, (n - O_LAG + 1) // GROUPS, mv2, ve2, rstd2, mv2_done, ve2_done, rstd2_done)
                rsqrt(b, NT - 1, mv2, ve2, rstd2, mv2_done, ve2_done, rstd2_done)

            def one_round(b, first=False, last=False):
                rope(b)
                pad_keys(b, first)
                attention(b)
                if not last:
                    ln1(b + 1)

            pool.wait_ge(attn_loaded, 16 * (N_CONST - 1))
            ln1(0)
            one_round(0, first=True)
            with pool.Fori(1, NB - 1) as b:
                one_round(b)
            one_round(NB - 1, last=True)



def rope_tables(np):
    inv_freq = (np.float32(1.0) / np.float32(10000.0)
                ** (np.arange(0, HD, 2, dtype=np.float32) / np.float32(HD))).astype(np.float32)
    freqs = np.outer(np.arange(SEQ, dtype=np.float32), inv_freq).astype(np.float32)
    emb = np.concatenate([freqs, freqs], -1)
    sign = np.where(np.arange(HD) % 2 == 0, -1.0, 1.0).astype(np.float32)
    cos = np.tile(np.cos(emb).T, (HPT, 1))
    sin = np.tile((np.sin(emb) * sign).T, (HPT, 1))
    return np.ascontiguousarray(np.stack([cos, sin], 1).astype(np.float32))


def masks(np):
    qi, kj = np.arange(P)[:, None], np.arange(P)[None, :]
    window = np.concatenate([np.where(kj >= qi, 0.0, NEG), np.where(kj <= qi, 0.0, NEG)], 1).astype(np.float32)
    rows = np.arange(P)
    headmask = (rows[:, None] // HD == np.arange(HPT)[None, :]).astype(np.float32)
    headmask4 = np.repeat(headmask, NGLOB, axis=1)
    gmask = np.zeros((P, 3, NGLOB), np.float32)
    gmask[:, 0, :] = np.where(rows[:, None] <= np.arange(NGLOB)[None, :], NEG, 0.0)
    even_odd = np.stack([(rows // HD) % 2 == 0, (rows // HD) % 2 == 1], 1).astype(np.float32)
    minus_half = np.full((P, 1), -0.5, np.float32)
    pick = np.zeros((P, UH * NGLOB), np.float32)
    pick[:NGLOB] = np.tile(np.eye(NGLOB, dtype=np.float32), (1, UH))
    vg = np.zeros((P, EMB), np.float32)
    vg[:UH * NGLOB] = (np.arange(UH * NGLOB)[:, None] // NGLOB == (np.arange(EMB)[None, :] % P) // 32)
    small = np.concatenate([np.eye(P, dtype=np.float32), headmask, headmask4, gmask.reshape(P, -1), even_odd,
                            minus_half, pick, vg], 1).astype(np.float32)
    return np.ascontiguousarray(window), np.ascontiguousarray(small)


def kernel(**inputs):
    import numpy as np
    import concourse.bacc as bacc
    from concourse.bass_utils import run_bass_kernel_spmd

    given = {n: np.asarray(a) for n, a in inputs.items()}

    def tiled(a):
        return np.ascontiguousarray(a.reshape(-1, P, a.shape[-1]).transpose(1, 0, 2))

    heads = np.arange(HEADS).reshape(NF, 2, UH).transpose(0, 2, 1).reshape(-1)
    order = (heads[:, None] * HD + np.arange(HD)[None, :]).reshape(-1)
    qkv = given["L0_attn_qkv_w"]
    qkv = np.concatenate([qkv[:2 * EMB], qkv[2 * EMB:][order]], 0)
    ffn_w = np.concatenate([tiled(given[f"L0_ffn_{n}_w"].T).reshape(P, -1) for n in ("w1", "w2", "h1", "h2", "w3")], 1)
    ffn_s = np.stack([given[f"L0_ffn_{n}_s"].reshape(NH, P).T for n in ("w1", "w2", "h1", "h2")], 1)
    window, small = masks(np)
    arrays = {
        "x": given["L0_attn_x"], "qkvT": tiled(qkv.T), "outT": tiled(given["L0_attn_out_w"].T[order]),
        "ffn_w": ffn_w, "ffn_s": ffn_s, "s3row": given["L0_ffn_w3_s"].reshape(1, EMB),
        "rope": rope_tables(np), "mask": window, "small": small,
    }
    nc = bacc.Bacc("TRN2", target_bir_lowering=False, num_devices=1)
    feed, args = {}, []
    for name, a in arrays.items():
        feed[f"in_{name}"] = np.ascontiguousarray(a)
        args.append(nc.dram_tensor(f"in_{name}", a.shape, mybir.dt.from_np(a.dtype), kind="ExternalInput").ap())
    args.append(nc.dram_tensor("y", (NB, SEQ, EMB), F32, kind="ExternalOutput").ap())
    layer_kernel(nc, *args)
    result = run_bass_kernel_spmd(nc, [feed], core_ids=[0])
    return result.results[0]["y"]
```

```python
import concourse.bass as bass
from concourse import mybir
from contextlib import ExitStack

F32 = mybir.dt.float32
F32R = mybir.dt.float32r
U16 = mybir.dt.uint16
I32 = mybir.dt.int32
ALU = mybir.AluOpType
ACT = mybir.ActivationFunctionType
AX = mybir.AxisListType

P = 128
NB, SEQ, EMB = 8, 512, 256
HEADS, HD = 16, 16
HID = 1024
NT = SEQ // P
NF = EMB // P
NH = HID // P
HPT = P // HD
NGLOB = 4
SCALE = HD ** -0.5
LN_EPS = 1e-5
NEG = -3.0e38

UH = 4
UNITS = NT * HEADS // UH
GROUPS = HEADS // UH
LATER = UNITS - GROUPS
FAR = UNITS - 2 * GROUPS
KEYS = 2 * P
COLS = KEYS + NGLOB
SM_RING = 3
STAT_RING = 4

T_LAG, PV_LAG = 2, 3
HEADS_LAG, O_LAG, RES_LAG, APPLY_LAG, TURN_LAG, SPLIT_LAG = 7, 8, 9, 10, 11, 12
STEPS = UNITS + PV_LAG
G_STEP = 2 * GROUPS - 2

W_UP, W_H1 = 0, 2 * NF * HID
W_H2 = W_H1 + NH * HID
W_DN = W_H2 + NH * HID
W_COLS = W_DN + NH * EMB
W_PARTS = [(W_UP, W_H1), (W_H1, W_H2), (W_H2, W_DN), (W_DN, W_COLS)]
CHECK = 2048
CHECKS = W_COLS // CHECK

LN1_TILE = 6

HALF = SEQ // 2
GATED = 2 * NH
DEEP = 2 * NH
FFN_TILES = GATED + DEEP
HALVES = 2 * UNITS
B6_USES = 1 + 2 * NT
B6_PROJECTED = (2, 4, 6, 8)


def tile_at(n, lag):
    i, rest = divmod(n - lag, GROUPS)
    return i if rest == 0 and 0 <= i < NT else None


def layer_kernel(nc, x, qkvT, outT, ffn_w, ffn_s, s3row, rope, mask, small, out):
    x_v = x.rearrange("b (t p) e -> b p t e", p=P)
    out_v = out.rearrange("b (t p) e -> b t p e", p=P)
    w_scratch = nc.dram_tensor("w_scratch", (P, W_COLS), F32, kind="Internal").ap()

    ctx = ExitStack()
    with ctx:
        def sem(name):
            return ctx.enter_context(nc.semaphore(name))

        base = (nc.sbuf_base + 31) // 32 * 32
        arena_bytes = (nc.sbuf_usable_end - base) // 32 * 32 - 64
        ctx.enter_context(nc.sbuf_tensor("arena", [P, arena_bytes // 4], F32))
        used = [base]

        def sb(name, shape, dt=F32, at=None):
            size = 4
            for n in shape[1:]:
                size *= n
            if at is None:
                at = used[0]
                used[0] = (at + size + 31) // 32 * 32
                assert used[0] <= base + arena_bytes, (name, used[0] - base, arena_bytes)
            return nc.alloc_sbuf_tensor_at(name, shape, dt, offset=at)

        W = sb("W", [P, W_COLS], F32R)
        a_at = used[0]
        a_hi = sb("a_hi", [P, NH, SEQ], F32R)
        a_lo = sb("a_lo", [P, NH, SEQ], F32R)
        b_at = used[0]
        b_hi = sb("b_hi", [P, NH, SEQ], F32R)
        b_lo = sb("b_lo", [P, NH, SEQ], F32R)
        Sm = sb("Sm", [P, SM_RING, UH, COLS], at=a_at)
        pt_at = a_at + SM_RING * UH * COLS * 4
        PT = sb("PT", [P, 2, 2, UH, P], at=pt_at)
        pg_at = pt_at + 2 * 2 * UH * P * 4
        PgT = sb("PgT", [UH * NGLOB, 2, P], at=pg_at)
        junk = sb("junk", [P, CHECK], at=pg_at + 2 * P * 4)
        assert pg_at + 2 * P * 4 + CHECK * 4 <= b_at
        Kz = sb("Kz", [P, HEADS, SEQ], at=b_at)
        x2_hi = sb("x2_hi", [P, NF, SEQ], F32R)
        x2_lo = sb("x2_lo", [P, NF, SEQ], F32R)
        x_in = sb("x_in", [P, NT, EMB])
        x_res = sb("x_res", [P, NT, EMB])
        featT = sb("featT", [P, NF, SEQ])
        q = sb("q", [P, NF, SEQ])
        k = sb("k", [P, NF, SEQ])
        v = sb("v", [P, NT, EMB])
        xn = sb("xn", [P, NT, EMB])
        rot = xn[:, :, :].rearrange("p (r t) e -> p r (t e)", r=2)
        silu = xn
        Vg = sb("Vg", [UH * NGLOB, EMB])
        Kg = sb("Kg", [P, NF, HPT, NGLOB])
        Pg = sb("Pg", [P, SM_RING, UH * NGLOB])
        Gs = sb("Gs", [P, 2, HEADS, NGLOB])
        gmax = sb("gmax", [P, 2, HEADS])
        mx = sb("mx", [P, STAT_RING, UH])
        negm = sb("negm", [P, STAT_RING, UH])
        rowsum = sb("rowsum", [P, STAT_RING, UH])
        rinv = sb("rinv", [P, STAT_RING, UH])
        bn1 = sb("bn1", [P, NT, 6])
        mv1 = sb("mv1", [P, NT, 2])
        ve1 = sb("ve1", [P, NT])
        rstd1 = sb("rstd1", [P, NT])
        bn2 = sb("bn2", [P, NT, 6])
        mv2 = sb("mv2", [P, NT, 2])
        ve2 = sb("ve2", [P, NT])
        rstd2 = sb("rstd2", [P, NT])
        low_sum = sb("low_sum", [P, CHECKS])
        low_all = sb("low_all", [P, 1])
        low_row = sb("low_row", [1, P])
        low_max = sb("low_max", [1, 1])
        low_int = sb("low_int", [1, 1], I32)
        qkv_w = sb("qkv_w", [P, NF, 3 * EMB])
        out_w = sb("out_w", [P, NF, EMB])
        scales = sb("scales", [P, 4, NH])
        s3 = sb("s3", [P, EMB])
        cos_sin = sb("cos_sin", [P, 2, SEQ])
        msk = sb("msk", [P, 2, KEYS])
        consts = sb("consts", [P, small.shape[1]])
        at = 0
        ident = consts[:, at:at + P]
        at += P
        headmask = consts[:, at:at + HPT]
        at += HPT
        even_odd = consts[:, at:at + 2]
        at += 2
        minus_half = consts[:, at:at + 1]
        at += 1
        pick_glob = consts[:, at:at + UH * NGLOB]
        at += UH * NGLOB
        vg_mask = consts[0:UH * NGLOB, at:at + UH]
        at += UH
        assert at == small.shape[1]

        bank = [ctx.enter_context(nc.psum_tensor(f"bank{i}", [P, 512], F32)) for i in range(8)]

        attn_loaded = sem("attn_loaded")
        scratch_written = [sem(f"scratch_written{n}") for n in range(len(W_PARTS))]
        w_loaded = [sem(f"w_loaded{n}") for n in range(len(W_PARTS))]
        x_loaded = sem("x_loaded")
        y_stored = sem("y_stored")
        low_moved = sem("low_moved")
        low_summed = sem("low_summed")
        low_found = sem("low_found")
        low_ready = sem("low_ready")
        bn1_done = sem("bn1_done")
        mv1_done = sem("mv1_done")
        ve1_done = sem("ve1_done")
        rstd1_done = sem("rstd1_done")
        xn1_done = sem("xn1_done")
        ln1_turned = sem("ln1_turned")
        xnT_done = sem("xnT_done")
        qk_done = sem("qk_done")
        rot_done = sem("rot_done")
        cos_done = sem("cos_done")
        sin_done = sem("sin_done")
        rope_done = sem("rope_done")
        v_done = sem("v_done")
        v_kept = sem("v_kept")
        vg_done = sem("vg_done")
        vg_kept = sem("vg_kept")
        down_done = sem("down_done")
        down_scaled = sem("down_scaled")
        y_done = sem("y_done")
        kz_low = sem("kz_low")
        kz_high = sem("kz_high")
        kg_done = sem("kg_done")
        g_done = sem("g_done")
        gs_done = sem("gs_done")
        b6_free = sem("b6_free")
        s_done = sem("s_done")
        s_free = sem("s_free")
        negm_done = sem("negm_done")
        exp_done = sem("exp_done")
        rinv_done = sem("rinv_done")
        norm_done = sem("norm_done")
        pg_done = sem("pg_done")
        cur_turned = sem("cur_turned")
        prev_turned = sem("prev_turned")
        glob_turned = sem("glob_turned")
        cur_kept = sem("cur_kept")
        prev_kept = sem("prev_kept")
        glob_kept = sem("glob_kept")
        pv_done = sem("pv_done")
        pv_even_kept = sem("pv_even_kept")
        pv_kept = sem("pv_kept")
        o_done = sem("o_done")
        x1_done = sem("x1_done")
        bn2_done = sem("bn2_done")
        mv2_done = sem("mv2_done")
        ve2_done = sem("ve2_done")
        rstd2_done = sem("rstd2_done")
        xn2_done = sem("xn2_done")
        ln2_turned = sem("ln2_turned")
        x2hi_done = sem("x2hi_done")
        gated_done = sem("gated_done")
        silu_done = sem("silu_done")
        mul_done = sem("mul_done")
        uphi_done = sem("uphi_done")
        deep_done = sem("deep_done")
        gelu_done = sem("gelu_done")
        ffn_free = sem("ffn_free")

        def at_round(b, per, n):
            return b * per + n

        block = ctx.enter_context(nc.Block())

        N_CONST = 8

        @block.sync
        def _(sp):
            def load_x(b):
                sp.dma_start(x_in[:, :, :], x_v[b]).then_inc(x_loaded, 16)

            def store_y(b):
                for t in range(NT):
                    sp.wait_ge(y_done, at_round(b, NT, t + 1))
                    sp.dma_start(out_v[b, t], x_res[:, t, :]).then_inc(y_stored, 16)

            def next_x(b):
                sp.wait_ge(x1_done, at_round(b, NT, NT))
                load_x(b + 1)

            load_x(0)
            sp.dma_start(consts[:, :], small).then_inc(attn_loaded, 16)
            sp.dma_start(qkv_w[:, :, :], qkvT).then_inc(attn_loaded, 16)
            sp.dma_start(cos_sin[:, :, :], rope).then_inc(attn_loaded, 16)
            sp.dma_start(msk[:, :, :], mask).then_inc(attn_loaded, 16)
            sp.dma_start(out_w[:, :, :], outT).then_inc(attn_loaded, 16)
            sp.dma_start(scales[:, :, :], ffn_s).then_inc(attn_loaded, 16)
            sp.dma_start(s3[:, :], s3row.broadcast_to([P, EMB])).then_inc(attn_loaded, 16)
            for n, (c0, c1) in enumerate(W_PARTS):
                sp.dma_start(w_scratch[:, c0:c1], ffn_w[:, c0:c1]).then_inc(scratch_written[n], 16)
            for n, (c0, c1) in enumerate(W_PARTS):
                sp.wait_ge(scratch_written[n], 16)
                sp.dma_start(W[:, c0:c1].bitcast(F32), w_scratch[:, c0:c1]).then_inc(w_loaded[n], 16)
            sp.wait_ge(low_found, 1)
            sp.dma_start(low_row[0:1, :].rearrange("a (p o) -> a p o", o=1), low_all[:, :])\
                .then_inc(low_moved, 16)

            next_x(0)
            with sp.Fori(1, NB - 1) as b:
                store_y(b - 1)
                next_x(b)
            store_y(NB - 2)
            store_y(NB - 1)
            sp.wait_ge(y_stored, 16 * NT * NB)

        @block.tensor
        def _(pe):
            def ln1_transposes(b):
                for t in range(NT):
                    pe.wait_ge(xn1_done, at_round(b, NT, t + 1))
                    for f in range(NF):
                        mm = nc.tensor.transpose(bank[4 + f][:, t * P:(t + 1) * P],
                                                 xn[:, t, f * P:(f + 1) * P], ident)
                        if t == NT - 1:
                            mm.then_inc(ln1_turned, 1)

            def qk_projection(b):
                pe.wait_ge(xnT_done, at_round(b, NF, NF))
                for n in range(2 * NF):
                    f, kind = n // 2, n % 2
                    col = kind * EMB + f * P
                    for kk in range(NF):
                        mm = nc.tensor.matmul(bank[[6, 7, 4, 5][n]][:, :], qkv_w[:, kk, col:col + P],
                                              featT[:, kk, :], start=(kk == 0), stop=(kk == NF - 1))
                    mm.then_inc(qk_done, 1)

            def v_projection(b):
                for t in range(NT):
                    pe.wait_ge(rot_done, at_round(b, 2 * NF, t + 1))
                    for kk in range(NF):
                        mm = nc.tensor.matmul(bank[[6, 7, 4, 5][t]][:, 0:EMB], featT[:, kk, t * P:(t + 1) * P],
                                              qkv_w[:, kk, 2 * EMB:3 * EMB], start=(kk == 0), stop=(kk == NF - 1))
                    mm.then_inc(v_done, 1)
                pe.wait_ge(v_kept, at_round(b, NT, 1))
                nc.tensor.matmul(bank[6][0:UH * NGLOB, 0:EMB], pick_glob, v[:, 0, :],
                                 start=True, stop=True).then_inc(vg_done, 1)

            def ffn_down(b, nxt, general):
                pe.wait_ge(ffn_free, at_round(b, FFN_TILES, FFN_TILES))
                for t in range(NT):
                    if nxt is not None:
                        if t < NT - 1:
                            pe.wait_ge(v_kept, at_round(nxt, NT, t + 2))
                        else:
                            pe.wait_ge(vg_kept, at_round(nxt, 1, 1))
                    for kk in range(NH):
                        for part, h in enumerate((a_hi, a_lo)):
                            lhsT = h[:, kk, t * P:(t + 1) * P]
                            rhs = W[:, W_DN + kk * EMB:W_DN + (kk + 1) * EMB]
                            if general:
                                lhsT, rhs = lhsT.bitcast(F32), rhs.bitcast(F32)
                            mm = nc.tensor.matmul(bank[[7, 4, 5, 6][t]][:, 0:EMB], lhsT, rhs,
                                                  start=(kk == 0 and part == 0), stop=(kk == NH - 1 and part == 1))
                    mm.then_inc(down_done, 1)

            def out_projection(b, i):
                pe.wait_ge(b6_free, at_round(b, B6_USES, B6_PROJECTED[i] - 1))
                pe.wait_ge(pv_kept, at_round(b, NT, i + 1))
                for f in range(NF):
                    mm = nc.tensor.matmul(bank[6][:, 0:EMB], featT[:, f, i * P:(i + 1) * P], out_w[:, f, :],
                                          start=(f == 0), stop=(f == NF - 1))
                mm.then_inc(o_done, 1)

            def ln2_transposes(b, i):
                pe.wait_ge(b6_free, at_round(b, B6_USES, B6_PROJECTED[i]))
                pe.wait_ge(xn2_done, at_round(b, NT, i + 1))
                for f in range(NF):
                    mm = nc.tensor.transpose(bank[6][:, f * P:(f + 1) * P], xn[:, i, f * P:(f + 1) * P], ident)
                mm.then_inc(ln2_turned, 1)

            def attention(b, first):
                def global_scores():
                    pe.wait_ge(kg_done, at_round(b, 1, 1))
                    for i in range(2):
                        for f in range(NF):
                            col = (i * NF + f) * HPT * NGLOB
                            mm = nc.tensor.matmul(bank[6][:, col:col + HPT * NGLOB],
                                                  q[:, f, (i + 2) * P:(i + 3) * P],
                                                  Kg[:, f, :, :].rearrange("p h j -> p (h j)"), start=True, stop=True)
                    mm.then_inc(g_done, 1)

                def scores(n):
                    i, g = n // GROUPS, n % GROUPS
                    if i == 0:
                        f = g * UH // HPT
                        pe.wait_ge(rope_done, at_round(b, 2 * NF, 2 * f + 1))
                        if f == 0:
                            pe.wait_ge(kz_low, at_round(b, HPT, UH * (g + 1)))
                        else:
                            pe.wait_ge(kz_high, at_round(b, HPT, UH * (g + 1) - HPT))
                    lo = 0 if i else P
                    for half in range(2):
                        hs = 2 * n + half
                        if hs >= 3:
                            pe.wait_ge(s_free, at_round(b, HALVES, hs - 2))
                        for c2 in range(2):
                            h = g * UH + 2 * half + c2
                            mm = nc.tensor.matmul(bank[hs % 3][:, c2 * KEYS + lo:(c2 + 1) * KEYS],
                                                  q[:, h // HPT, i * P:(i + 1) * P],
                                                  Kz[:, h, i * P + lo - P:(i + 1) * P], start=True, stop=True)
                        mm.then_inc(s_done, 1)

                def transposes(n):
                    i = n // GROUPS
                    pe.wait_ge(norm_done, at_round(b, UNITS, n + 1))
                    if n:
                        pe.wait_ge(cur_kept, at_round(b, UNITS, n))
                    elif not first:
                        pe.wait_ge(y_done, at_round(b, NT, 0))
                    for c in range(UH):
                        mm = nc.tensor.transpose(bank[5][:, c * P:(c + 1) * P], Sm[:, n % SM_RING, c, P:KEYS], ident)
                    mm.then_inc(cur_turned, 1)
                    if i == 0:
                        return
                    m = n - GROUPS
                    if m:
                        pe.wait_ge(prev_kept, at_round(b, LATER, m))
                    for c in range(UH):
                        mm = nc.tensor.transpose(bank[4][:, c * P:(c + 1) * P], Sm[:, n % SM_RING, c, 0:P], ident)
                    mm.then_inc(prev_turned, 1)
                    if i == 1:
                        return
                    m = n - 2 * GROUPS
                    if m:
                        pe.wait_ge(glob_kept, at_round(b, FAR, m))
                    pe.wait_ge(pg_done, at_round(b, FAR, m + 1))
                    nc.tensor.transpose(bank[3][0:UH * NGLOB, 0:P], Pg[:, n % SM_RING, :], ident)\
                        .then_inc(glob_turned, 1)

                def weighted_values(n):
                    i, g = n // GROUPS, n % GROUPS
                    f = g * UH // HPT
                    pe.wait_ge(cur_kept, at_round(b, UNITS, n + 1))
                    if i:
                        pe.wait_ge(prev_kept, at_round(b, LATER, n - GROUPS + 1))
                        if i > 1:
                            pe.wait_ge(glob_kept, at_round(b, FAR, n - 2 * GROUPS + 1))
                        if g == 0:
                            pe.wait_ge(pv_kept, at_round(b, NT, i))
                    for side in ((1, 0) if i else (1,)):
                        for c in range(UH):
                            col = f * P + 32 * c
                            mm = nc.tensor.matmul(bank[7][32 * c:32 * c + 32, g * P:(g + 1) * P],
                                                  v[:, i - 1 + side, col:col + 32], PT[:, n % 2, side, c, :],
                                                  start=(side == 1), stop=(side == (0 if i == 1 else 1) and i < 2),
                                                  skip_group_check=True)
                    if i > 1:
                        mm = nc.tensor.matmul(bank[7][:, g * P:(g + 1) * P], Vg[:, f * P:(f + 1) * P],
                                              PgT[:, n % 2, :], start=False, stop=True, skip_group_check=True)
                    mm.then_inc(pv_done, 1)

                pe.wait_ge(v_kept, at_round(b, NT, NT))
                pe.wait_ge(vg_kept, at_round(b, 1, 1))
                if not first:
                    pe.wait_ge(ffn_free, at_round(b, FFN_TILES, 0))
                for n in range(STEPS):
                    if n < UNITS:
                        scores(n)
                    if 0 <= n - T_LAG < UNITS:
                        transposes(n - T_LAG)
                    if 0 <= n - PV_LAG < UNITS:
                        weighted_values(n - PV_LAG)
                    if n == G_STEP:
                        global_scores()
                    if (i := tile_at(n, O_LAG)) is not None:
                        out_projection(b, i)
                    if (i := tile_at(n, TURN_LAG)) is not None:
                        ln2_transposes(b, i)

            def ffn_tile(out, w_at, width, m, h_hi, h_lo, tiles, general, wait=None):
                for kk in range(tiles):
                    if wait is not None:
                        wait(kk)
                    lhsT = W[:, w_at + kk * width + m * P:w_at + kk * width + (m + 1) * P]
                    if general:
                        lhsT = lhsT.bitcast(F32)
                    for part, h in enumerate((h_hi, h_lo)):
                        rhs = h[:, kk, :].bitcast(F32) if general else h[:, kk, :]
                        mm = nc.tensor.matmul(out, lhsT, rhs, start=(kk == 0 and part == 0),
                                              stop=(kk == tiles - 1 and part == 1))
                return mm

            def gated_tile(b, s, general):
                half, m = s // NH, s % NH
                if s == 0:
                    pe.wait_ge(s_free, at_round(b, HALVES, HALVES))
                    pe.wait_ge(glob_kept, at_round(b, FAR, FAR))
                if m == 0:
                    pe.wait_ge(x2hi_done, at_round(b, NT, NT // 2 * (half + 1)))
                    pe.wait_ge(b6_free, at_round(b, B6_USES, B6_PROJECTED[NT // 2 * (half + 1) - 1] + 1))
                if s >= 4:
                    pe.wait_ge(ffn_free, at_round(b, FFN_TILES, s - 3))
                for u in range(2):
                    mm = ffn_tile(bank[s % 4][:, u * HALF:(u + 1) * HALF], W_UP + u * NF * HID, HID, m,
                                  x2_hi[:, :, half * HALF:(half + 1) * HALF],
                                  x2_lo[:, :, half * HALF:(half + 1) * HALF], NF, general)
                mm.then_inc(gated_done, 1)

            def ffn_hidden(b, general, last):
                between = {0: lambda: ln2_transposes(b, NT - 2), 2: lambda: out_projection(b, NT - 1),
                           6: lambda: ln2_transposes(b, NT - 1)}
                for s in range(GATED):
                    if s in between:
                        between[s]()
                    gated_tile(b, s, general)
                for layer, (w_at, h_hi, h_lo) in enumerate(((W_H1, a_hi, a_lo), (W_H2, b_hi, b_lo))):
                    for m in range(NH):
                        before = GATED + NH * layer
                        pe.wait_ge(ffn_free, at_round(b, FFN_TILES, before + m - 3))
                        if layer == 1 and m == LN1_TILE and not last:
                            ln1_transposes(b + 1)
                        wait = None
                        if m == 0:
                            def wait(kk, before=before):
                                if kk >= NH - 4:
                                    pe.wait_ge(ffn_free, at_round(b, FFN_TILES, before - NH + kk + 1))
                        ffn_tile(bank[m % 4][:, :], w_at, HID, m, h_hi, h_lo, NH, general, wait)\
                            .then_inc(deep_done, 1)

            pe.wait_ge(attn_loaded, 16 * (N_CONST - 1))
            ln1_transposes(0)
            qk_projection(0)
            v_projection(0)
            attention(0, True)
            pe.wait_ge(low_ready, 1)
            low_bits = pe.value_load(low_int[0:1, 0:1], min_val=0, max_val=1)

            def rounds(general):
                def one_round(b, last=False):
                    qk_projection(b)
                    v_projection(b)
                    ffn_down(b - 1, b, general)
                    attention(b, False)
                    ffn_hidden(b, general, last)

                ffn_hidden(0, general, False)
                with pe.Fori(1, NB - 1) as b:
                    one_round(b)
                one_round(NB - 1, last=True)
                ffn_down(NB - 1, None, general)

            with pe.If(low_bits):
                rounds(True)
            with pe.Else():
                rounds(False)

        @block.scalar
        def _(act):
            def keep_xnT(b):
                for f in range(NF):
                    act.wait_ge(ln1_turned, at_round(b, NF, f + 1))
                    nc.scalar.copy(featT[:, f, :], bank[4 + f][:, :]).then_inc(xnT_done, 1)

            def keep_v(b):
                for t in range(NT):
                    act.wait_ge(v_done, at_round(b, NT, t + 1))
                    nc.scalar.copy(v[:, t, :], bank[[6, 7, 4, 5][t]][:, 0:EMB]).then_inc(v_kept, 1)

            def keep_even_heads(b, i):
                act.wait_ge(pv_done, at_round(b, UNITS, GROUPS * (i + 1)))
                nc.scalar.activation(featT[:, :, i * P:(i + 1) * P],
                                     bank[7][:, :].rearrange("p (f s q) -> p f s q", f=NF, s=2)[:, :, 0, :],
                                     ACT.Copy, scale=even_odd[:, 0:1]).then_inc(pv_even_kept, 1)

            def keep_x2hi(b, i):
                act.wait_ge(ln2_turned, at_round(b, NT, i + 1))
                nc.scalar.copy(x2_hi[:, :, i * P:(i + 1) * P],
                               bank[6][:, 0:EMB].rearrange("p (f q) -> p f q", f=NF)).then_inc(x2hi_done, 1)

            def attention(b, first):
                def exponentials(n):
                    i, r = n // GROUPS, n % STAT_RING
                    c0, c1 = (0 if i else P), (COLS if i > 1 else KEYS)
                    act.wait_ge(negm_done, at_round(b, UNITS, n + 1))
                    for c in range(UH):
                        row = Sm[:, n % SM_RING, c, c0:c1]
                        ex = nc.scalar.activation(row, row, ACT.Exp, bias=negm[:, r, c:c + 1], scale=SCALE,
                                                  accum_out=rowsum[:, r, c:c + 1])
                    ex.then_inc(exp_done, 1)

                def keep_prev(n):
                    act.wait_ge(prev_turned, at_round(b, LATER, n - GROUPS + 1))
                    act.wait_ge(pv_done, at_round(b, UNITS, n - 1))
                    nc.scalar.copy(PT[:, n % 2, 0, :, :].rearrange("p c q -> p (c q)"), bank[4][:, :])\
                        .then_inc(prev_kept, 1)

                for n in range(STEPS):
                    if (i := tile_at(n, HEADS_LAG)) is not None:
                        keep_even_heads(b, i)
                    if (i := tile_at(n, SPLIT_LAG)) is not None:
                        keep_x2hi(b, i)
                    if n < UNITS:
                        exponentials(n)
                    if GROUPS <= n - T_LAG < UNITS:
                        keep_prev(n - T_LAG)
                    if first and n >= STEPS - CHECKS:
                        check_weights(n - (STEPS - CHECKS))

            def check_weights(n):
                c1 = (n + 1) * CHECK
                part = [c1 <= end for _, end in W_PARTS].index(True)
                act.wait_ge(w_loaded[part], 16)
                if n:
                    act.wait_ge(low_summed, n)
                nc.scalar.activation(junk[:, :], W[:, c1 - CHECK:c1].bitcast(U16)[:, 0:2 * CHECK:2], ACT.Copy,
                                     accum_out=low_sum[:, n:n + 1]).then_inc(low_summed, 1)

            def ffn_hidden(b, last):
                def up_hi(s):
                    half, m = s // NH, s % NH
                    act.wait_ge(mul_done, at_round(b, GATED, s + 1))
                    nc.scalar.copy(a_hi[:, m, half * HALF:(half + 1) * HALF], bank[s % 4][:, HALF:SEQ])\
                        .then_inc(uphi_done, 1)

                keep_even_heads(b, NT - 1)
                keep_x2hi(b, NT - 2)
                for s in range(GATED):
                    act.wait_ge(gated_done, at_round(b, GATED, s + 1))
                    if s >= 2:
                        act.wait_ge(mul_done, at_round(b, GATED, s - 1))
                    nc.scalar.activation(silu[:, s % 2, :], bank[s % 4][:, 0:HALF], ACT.Silu,
                                         scale=scales[:, 0, s % NH:s % NH + 1]).then_inc(silu_done, 1)
                    if s:
                        up_hi(s - 1)
                    if s == 5:
                        keep_x2hi(b, NT - 1)
                up_hi(GATED - 1)
                for n in range(DEEP):
                    layer, m = n // NH, n % NH
                    h_hi = (b_hi, a_hi)[layer]
                    ps = bank[m % 4][:, :]
                    s = scales[:, 2 + layer, m:m + 1]
                    if n == NH + LN1_TILE and not last:
                        keep_xnT(b + 1)
                    act.wait_ge(deep_done, at_round(b, DEEP, n + 1))
                    nc.scalar.activation(h_hi[:, m, :], ps, ACT.Gelu, scale=s)
                    nc.scalar.activation(ps, ps, ACT.Gelu, scale=s).then_inc(gelu_done, 1)

            act.wait_ge(attn_loaded, 16 * (N_CONST - 1))
            keep_xnT(0)
            keep_v(0)
            attention(0, True)
            ffn_hidden(0, False)
            with act.Fori(1, NB - 1) as b:
                keep_v(b)
                attention(b, False)
                ffn_hidden(b, False)
            keep_v(NB - 1)
            attention(NB - 1, False)
            ffn_hidden(NB - 1, True)

        @block.vector
        def _(dve):
            def ln1_stats(b, t):
                if t == 0:
                    dve.wait_ge(x_loaded, at_round(b, 16, 16))
                nc.vector.bn_stats(bn1[:, t, :], x_in[:, t, :]).then_inc(bn1_done, 1)
                dve.wait_ge(bn1_done, at_round(b, NT, t + 1))
                dve.nop(nofuse=True)
                nc.vector.bn_aggr(mv1[:, t, :], bn1[:, t, :]).then_inc(mv1_done, 1)

            def ln1_apply(b, t):
                dve.wait_ge(rstd1_done, at_round(b, NT, t + 1))
                nc.vector.tensor_scalar(xn[:, t, :], x_in[:, t, :], mv1[:, t, 0:1], rstd1[:, t:t + 1],
                                        ALU.subtract, ALU.mult).then_inc(xn1_done, 1)

            def rope(b):
                for n in range(2 * NF):
                    src = bank[[6, 7, 4, 5][n]]
                    dst = (q, k)[n % 2][:, n // 2, :]
                    dve.wait_ge(qk_done, at_round(b, 2 * NF, n + 1))
                    if n >= 2:
                        dve.wait_ge(rope_done, at_round(b, 2 * NF, n - 1))
                    nc.vector.tensor_tensor(dst, src[:, :], cos_sin[:, 0, :], ALU.mult).then_inc(cos_done, 1)
                    nc.vector.stream_shuffle(rot[:, n % 2, :], src[:, :], [p ^ 1 for p in range(32)])\
                        .then_inc(rot_done, 1)

            def keep_vg(b):
                dve.wait_ge(vg_done, at_round(b, 1, 1))
                nc.vector.tensor_tensor(
                    Vg[:, :].rearrange("p (f c d) -> p f c d", f=NF, c=UH),
                    bank[6][0:UH * NGLOB, 0:EMB].rearrange("p (f c d) -> p f c d", f=NF, c=UH),
                    vg_mask.unsqueeze(1).unsqueeze(3).broadcast_to([UH * NGLOB, NF, UH, P // UH]), ALU.mult)\
                    .then_inc(vg_kept, 1)

            def pad_keys(b, h0, first):
                if h0 == 0:
                    dve.wait_ge(rope_done, at_round(b, 2 * NF, 2))
                    if not first:
                        dve.wait_ge(deep_done, at_round(b, DEEP, 0))
                for h in range(h0, h0 + UH):
                    nc.vector.tensor_scalar(Kz[:, h, :], k[:, 0, :], headmask[:, h:h + 1], None, ALU.mult)\
                        .then_inc(kz_low, 1)

            def global_keys(b):
                dve.wait_ge(rope_done, at_round(b, 2 * NF, 2 * NF))
                nc.vector.tensor_tensor(
                    Kg[:, :, :, :], k[:, :, 0:NGLOB].unsqueeze(2).broadcast_to([P, NF, HPT, NGLOB]),
                    headmask.unsqueeze(1).unsqueeze(3).broadcast_to([P, NF, HPT, NGLOB]), ALU.mult).then_inc(kg_done, 1)

            def finish_y(b):
                for t in range(NT):
                    ps = bank[[7, 4, 5, 6][t]][:, 0:EMB]
                    dve.wait_ge(down_done, at_round(b, NT, t + 1))
                    nc.vector.tensor_tensor(ps, ps, s3[:, :], ALU.mult).then_inc(down_scaled, 1)
                    dve.wait_ge(down_scaled, at_round(b, NT, t + 1))
                    nc.vector.tensor_tensor(x_res[:, t, :], x_res[:, t, :], ps, ALU.add).then_inc(y_done, 1)

            def keep_odd_heads(b, i):
                dve.wait_ge(pv_even_kept, at_round(b, NT, i + 1))
                dst = featT[:, :, i * P:(i + 1) * P]
                nc.vector.scalar_tensor_tensor(
                    dst, bank[7][:, :].rearrange("p (f s q) -> p f s q", f=NF, s=2)[:, :, 1, :],
                    even_odd[:, 1:2], dst, ALU.mult, ALU.add).then_inc(pv_kept, 1)

            def residual(b, i):
                dve.wait_ge(o_done, at_round(b, NT, i + 1))
                if i == 0 and not (isinstance(b, int) and b == 0):
                    dve.wait_ge(y_stored, at_round(b, 16 * NT, 0))
                nc.vector.tensor_tensor(x_res[:, i, :], x_in[:, i, :], bank[6][:, 0:EMB], ALU.add)\
                    .then_inc(b6_free, 1)
                dve.wait_ge(b6_free, at_round(b, B6_USES, B6_PROJECTED[i]))
                nc.vector.bn_stats(bn2[:, i, :], x_res[:, i, :]).then_inc(x1_done, 1)
                dve.wait_ge(x1_done, at_round(b, NT, i + 1))
                dve.nop(nofuse=True)
                nc.vector.bn_aggr(mv2[:, i, :], bn2[:, i, :]).then_inc(mv2_done, 1)

            def ln2_apply(b, i):
                dve.wait_ge(rstd2_done, at_round(b, NT, i + 1))
                nc.vector.tensor_scalar(xn[:, i, :], x_res[:, i, :], mv2[:, i, 0:1], rstd2[:, i:i + 1],
                                        ALU.subtract, ALU.mult).then_inc(xn2_done, 1)

            def keep_x2lo(b, i):
                dve.wait_ge(x2hi_done, at_round(b, NT, i + 1))
                nc.vector.tensor_tensor(
                    x2_lo[:, :, i * P:(i + 1) * P], bank[6][:, 0:EMB].rearrange("p (f q) -> p f q", f=NF),
                    x2_hi[:, :, i * P:(i + 1) * P].bitcast(F32), ALU.subtract).then_inc(b6_free, 1)

            def attention(b, first):
                def global_scores():
                    dve.wait_ge(g_done, at_round(b, 1, 1))
                    nc.vector.tensor_copy(Gs[:, :, :, :].rearrange("p i h j -> p (i h j)"),
                                          bank[6][:, 0:2 * HEADS * NGLOB]).then_inc(b6_free, 1)
                    dve.wait_ge(b6_free, at_round(b, B6_USES, 1))
                    nc.vector.tensor_reduce(gmax[:, :, :].rearrange("p i h -> p (i h)"),
                                            Gs[:, :, :, :].rearrange("p i h j -> p (i h) j"),
                                            AX.X, ALU.max).then_inc(gs_done, 1)

                def masked_max(n):
                    i, g, r = n // GROUPS, n % GROUPS, n % STAT_RING
                    lo = 0 if i else P
                    buf = Sm[:, n % SM_RING, :, :]
                    if n >= SM_RING:
                        m = n - SM_RING
                        if m < GROUPS:
                            dve.wait_ge(cur_turned, at_round(b, UNITS, m + 1))
                        else:
                            dve.wait_ge(prev_turned, at_round(b, LATER, m - GROUPS + 1))
                    if n == 2 * GROUPS:
                        dve.wait_ge(gs_done, at_round(b, 1, 1))
                    if i > 1:
                        nc.vector.tensor_copy(buf[:, :, KEYS:COLS], Gs[:, i - 2, g * UH:(g + 1) * UH, :])
                    for half in range(2):
                        hs = 2 * n + half
                        dve.wait_ge(s_done, at_round(b, HALVES, hs + 1))
                        dve.nop(nofuse=True)
                        for c2 in range(2):
                            c = 2 * half + c2
                            h = g * UH + c
                            tt = nc.vector.tensor_tensor_reduce(
                                out=buf[:, c, lo:KEYS], in0=bank[hs % 3][:, c2 * KEYS + lo:(c2 + 1) * KEYS],
                                in1=msk[:, int(i == 1), lo:KEYS], scale=1.0,
                                scalar=gmax[:, i - 2, h:h + 1] if i > 1 else NEG,
                                op0=ALU.add, op1=ALU.max, accum_out=mx[:, r, c:c + 1])
                        tt.then_inc(s_free, 1)
                    dve.wait_ge(s_free, at_round(b, HALVES, 2 * n + 2))
                    nc.vector.tensor_scalar(negm[:, r, :], mx[:, r, :], -SCALE, None, ALU.mult).then_inc(negm_done, 1)

                def inverse_sums(n):
                    r = n % STAT_RING
                    dve.wait_ge(exp_done, at_round(b, UNITS, n + 1))
                    nc.vector.reciprocal(rinv[:, r, :], rowsum[:, r, :]).then_inc(rinv_done, 1)

                def keep_cur(n):
                    dve.wait_ge(cur_turned, at_round(b, UNITS, n + 1))
                    if n >= 2:
                        dve.wait_ge(pv_done, at_round(b, UNITS, n - 1))
                    nc.vector.tensor_copy(PT[:, n % 2, 1, :, :].rearrange("p c q -> p (c q)"), bank[5][:, :])\
                        .then_inc(cur_kept, 1)
                    if n >= 2 * GROUPS:
                        dve.wait_ge(glob_turned, at_round(b, FAR, n - 2 * GROUPS + 1))
                        nc.vector.tensor_copy(PgT[:, n % 2, :], bank[3][0:UH * NGLOB, 0:P]).then_inc(glob_kept, 1)

                for n in range(STEPS):
                    if n < UNITS:
                        masked_max(n)
                    if (i := tile_at(n, HEADS_LAG)) is not None:
                        keep_odd_heads(b, i)
                    if 0 <= n - 1 < UNITS:
                        inverse_sums(n - 1)
                    if 0 <= n - T_LAG < UNITS:
                        keep_cur(n - T_LAG)
                    if n == G_STEP + 1:
                        global_scores()
                    for lag, stage in ((SPLIT_LAG, keep_x2lo), (RES_LAG, residual), (APPLY_LAG, ln2_apply)):
                        if (i := tile_at(n, lag)) is not None:
                            stage(b, i)
                if first:
                    low_bits()

            def low_bits():
                dve.wait_ge(low_summed, CHECKS)
                nc.vector.tensor_reduce(low_all[:, :], low_sum[:, :], AX.X, ALU.max).then_inc(low_found, 1)
                dve.wait_ge(low_moved, 16)
                nc.vector.tensor_reduce(low_max[:, :], low_row[:, :], AX.X, ALU.max).then_inc(low_found, 1)
                dve.wait_ge(low_found, 2)
                nc.vector.tensor_scalar(low_int[:, :], low_max[:, :], 0.0, None, ALU.is_gt).then_inc(low_ready, 1)

            def ffn_hidden(b, last):
                def up_lo(s):
                    half, m = s // NH, s % NH
                    cols = slice(half * HALF, (half + 1) * HALF)
                    dve.wait_ge(uphi_done, at_round(b, GATED, s + 1))
                    nc.vector.tensor_tensor(a_lo[:, m, cols], bank[s % 4][:, HALF:SEQ],
                                            a_hi[:, m, cols].bitcast(F32), ALU.subtract).then_inc(ffn_free, 1)

                keep_odd_heads(b, NT - 1)
                keep_x2lo(b, NT - 2)
                for s in range(GATED):
                    up = bank[s % 4][:, HALF:SEQ]
                    dve.wait_ge(silu_done, at_round(b, GATED, s + 1))
                    nc.vector.scalar_tensor_tensor(up, up, scales[:, 1, s % NH:s % NH + 1], silu[:, s % 2, :],
                                                   ALU.mult, ALU.mult).then_inc(mul_done, 1)
                    if s:
                        up_lo(s - 1)
                    for at, stage in ((1, residual), (3, ln2_apply), (5, keep_x2lo)):
                        if s == at:
                            stage(b, NT - 1)
                up_lo(GATED - 1)
                for n in range(DEEP):
                    layer, m = n // NH, n % NH
                    h_hi, h_lo = ((b_hi, b_lo), (a_hi, a_lo))[layer]
                    dve.wait_ge(gelu_done, at_round(b, DEEP, n + 1))
                    nc.vector.tensor_tensor(h_lo[:, m, :], bank[m % 4][:, :], h_hi[:, m, :].bitcast(F32),
                                            ALU.subtract).then_inc(ffn_free, 1)
                    if not last:
                        if 2 <= n < 2 + NT:
                            ln1_stats(b + 1, n - 2)
                        if 6 <= n < 6 + NT:
                            ln1_apply(b + 1, n - 6)

            def one_round(b, first=False, last=False):
                rope(b)
                keep_vg(b)
                pad_keys(b, 0, first)
                pad_keys(b, UH, first)
                global_keys(b)
                if not first:
                    finish_y(b - 1)
                attention(b, first)
                ffn_hidden(b, last)

            for t in range(NT):
                ln1_stats(0, t)
            for t in range(NT):
                ln1_apply(0, t)
            dve.wait_ge(attn_loaded, 16 * (N_CONST - 1))
            one_round(0, first=True)
            with dve.Fori(1, NB - 1) as b:
                one_round(b)
            one_round(NB - 1, last=True)
            finish_y(NB - 1)

        @block.gpsimd
        def _(pool):
            def rsqrt(b, t, mv, ve, rstd, stats, ve_done, done):
                pool.wait_ge(stats, at_round(b, NT, t + 1))
                pool.nop(nofuse=True)
                nc.gpsimd.tensor_scalar(ve[:, t:t + 1], mv[:, t, 1:2], LN_EPS, None, ALU.add).then_inc(ve_done, 1)
                pool.wait_ge(ve_done, at_round(b, NT, t + 1))
                nc.gpsimd.tensor_tensor(rstd[:, t:t + 1], ve[:, t:t + 1], minus_half, ALU.pow).then_inc(done, 1)

            def ln1(b):
                for t in range(NT):
                    rsqrt(b, t, mv1, ve1, rstd1, mv1_done, ve1_done, rstd1_done)

            def rope(b):
                for n in range(2 * NF):
                    dst = (q, k)[n % 2][:, n // 2, :]
                    pool.wait_ge(rot_done, at_round(b, 2 * NF, n + 1))
                    nc.gpsimd.tensor_tensor(rot[:, n % 2, :], rot[:, n % 2, :], cos_sin[:, 1, :], ALU.mult)\
                        .then_inc(sin_done, 1)
                    pool.wait_ge(sin_done, at_round(b, 2 * NF, n + 1))
                    pool.wait_ge(cos_done, at_round(b, 2 * NF, n + 1))
                    nc.gpsimd.tensor_tensor(dst, dst, rot[:, n % 2, :], ALU.add).then_inc(rope_done, 1)

            def pad_keys(b, first):
                pool.wait_ge(rope_done, at_round(b, 2 * NF, 2 * NF))
                if not first:
                    pool.wait_ge(deep_done, at_round(b, DEEP, 0))
                pool.nop(nofuse=True)
                for h in range(HPT):
                    nc.gpsimd.tensor_scalar(Kz[:, HPT + h, :], k[:, 1, :], headmask[:, h:h + 1], 1.0,
                                            ALU.mult, ALU.mult).then_inc(kz_high, 1)

            def attention(b):
                for n in range(UNITS):
                    i, r = n // GROUPS, n % STAT_RING
                    c0, c1 = (0 if i else P), KEYS
                    pool.wait_ge(rinv_done, at_round(b, UNITS, n + 1))
                    if i > 1:
                        nc.gpsimd.tensor_tensor(
                            Pg[:, n % SM_RING, :].rearrange("p (c j) -> p c j", j=NGLOB),
                            Sm[:, n % SM_RING, :, KEYS:COLS],
                            rinv[:, r, :].unsqueeze(2).broadcast_to([P, UH, NGLOB]), ALU.mult).then_inc(pg_done, 1)
                    rows = Sm[:, n % SM_RING, :, c0:c1]
                    nc.gpsimd.tensor_tensor(rows, rows, rinv[:, r, :].unsqueeze(2).broadcast_to([P, UH, c1 - c0]),
                                            ALU.mult).then_inc(norm_done, 1)
                    if (t := tile_at(n, RES_LAG - 1)) is not None:
                        rsqrt(b, t, mv2, ve2, rstd2, mv2_done, ve2_done, rstd2_done)
                for t in (NT - 2, NT - 1):
                    rsqrt(b, t, mv2, ve2, rstd2, mv2_done, ve2_done, rstd2_done)

            def one_round(b, first=False, last=False):
                rope(b)
                pad_keys(b, first)
                attention(b)
                if not last:
                    ln1(b + 1)

            pool.wait_ge(attn_loaded, 16 * (N_CONST - 1))
            ln1(0)
            one_round(0, first=True)
            with pool.Fori(1, NB - 1) as b:
                one_round(b)
            one_round(NB - 1, last=True)



def rope_tables(np):
    inv_freq = (np.float32(1.0) / np.float32(10000.0)
                ** (np.arange(0, HD, 2, dtype=np.float32) / np.float32(HD))).astype(np.float32)
    freqs = np.outer(np.arange(SEQ, dtype=np.float32), inv_freq).astype(np.float32)
    emb = np.concatenate([freqs, freqs], -1)
    sign = np.where(np.arange(HD) % 2 == 0, -1.0, 1.0).astype(np.float32)
    cos = np.tile(np.cos(emb).T, (HPT, 1))
    sin = np.tile((np.sin(emb) * sign).T, (HPT, 1))
    return np.ascontiguousarray(np.stack([cos, sin], 1).astype(np.float32))


def masks(np):
    qi, kj = np.arange(P)[:, None], np.arange(P)[None, :]
    before, own = np.where(kj >= qi, 0.0, NEG), np.where(kj <= qi, 0.0, NEG)
    before_1 = np.where((kj >= qi) | (kj < NGLOB), 0.0, NEG)
    window = np.stack([np.concatenate([before, own], 1), np.concatenate([before_1, own], 1)], 1).astype(np.float32)
    rows = np.arange(P)
    headmask = (rows[:, None] // HD == np.arange(HPT)[None, :]).astype(np.float32)
    even_odd = np.stack([(rows // HD) % 2 == 0, (rows // HD) % 2 == 1], 1).astype(np.float32)
    minus_half = np.full((P, 1), -0.5, np.float32)
    pick = np.zeros((P, UH * NGLOB), np.float32)
    pick[:NGLOB] = np.tile(np.eye(NGLOB, dtype=np.float32), (1, UH))
    vg = np.zeros((P, UH), np.float32)
    vg[:UH * NGLOB] = np.arange(UH * NGLOB)[:, None] // NGLOB == np.arange(UH)[None, :]
    small = np.concatenate([np.eye(P, dtype=np.float32), headmask, even_odd,
                            minus_half, pick, vg], 1).astype(np.float32)
    return np.ascontiguousarray(window), np.ascontiguousarray(small)


def kernel(**inputs):
    import numpy as np
    import concourse.bacc as bacc
    from concourse.bass_utils import run_bass_kernel_spmd

    given = {n: np.asarray(a) for n, a in inputs.items()}

    def tiled(a):
        return np.ascontiguousarray(a.reshape(-1, P, a.shape[-1]).transpose(1, 0, 2))

    heads = np.arange(HEADS).reshape(NF, 2, UH).transpose(0, 2, 1).reshape(-1)
    order = (heads[:, None] * HD + np.arange(HD)[None, :]).reshape(-1)
    qkv = given["L0_attn_qkv_w"]
    qkv = np.concatenate([qkv[:2 * EMB], qkv[2 * EMB:][order]], 0)
    ffn_w = np.concatenate([tiled(given[f"L0_ffn_{n}_w"].T).reshape(P, -1) for n in ("w1", "w2", "h1", "h2", "w3")], 1)
    ffn_s = np.stack([given[f"L0_ffn_{n}_s"].reshape(NH, P).T for n in ("w1", "w2", "h1", "h2")], 1)
    window, small = masks(np)
    arrays = {
        "x": given["L0_attn_x"], "qkvT": tiled(qkv.T), "outT": tiled(given["L0_attn_out_w"].T[order]),
        "ffn_w": ffn_w, "ffn_s": ffn_s, "s3row": given["L0_ffn_w3_s"].reshape(1, EMB),
        "rope": rope_tables(np), "mask": window, "small": small,
    }
    nc = bacc.Bacc("TRN2", target_bir_lowering=False, num_devices=1)
    feed, args = {}, []
    for name, a in arrays.items():
        feed[f"in_{name}"] = np.ascontiguousarray(a)
        args.append(nc.dram_tensor(f"in_{name}", a.shape, mybir.dt.from_np(a.dtype), kind="ExternalInput").ap())
    args.append(nc.dram_tensor("y", (NB, SEQ, EMB), F32, kind="ExternalOutput").ap())
    layer_kernel(nc, *args)
    result = run_bass_kernel_spmd(nc, [feed], core_ids=[0])
    return result.results[0]["y"]
```

```python
import concourse.bass as bass
from concourse import mybir
from contextlib import ExitStack

F32 = mybir.dt.float32
F32R = mybir.dt.float32r
U16 = mybir.dt.uint16
I32 = mybir.dt.int32
ALU = mybir.AluOpType
ACT = mybir.ActivationFunctionType
AX = mybir.AxisListType

P = 128
NB, SEQ, EMB = 8, 512, 256
HEADS, HD = 16, 16
HID = 1024
NT = SEQ // P
NF = EMB // P
NH = HID // P
HPT = P // HD
NGLOB = 4
SCALE = HD ** -0.5
LN_EPS = 1e-5
FAR_OFF = 3.0e38

UH = 4
UNITS = NT * HEADS // UH
GROUPS = HEADS // UH
LATER = UNITS - GROUPS
FAR = UNITS - 2 * GROUPS
KEYS = 2 * P
COLS = KEYS + NGLOB
SM_RING = 4
PARTS = 4
PAIRS = HEADS // 2
SPLIT_SCALE = (-SCALE, 1.0)
Q_PARTS, K_PARTS = (0, 0, 1, 1), (2, 3, 2, 3)
SAVES = PARTS
LOADS = 2 * NF
STAT_RING = 4

T_LAG, PV_LAG = 2, 3
SPREAD_LAG, HEADS_LAG, O_LAG, RES_LAG, TURN_LAG, SPLIT_LAG = 5, 7, 8, 9, 11, 11
LAST_RES = RES_LAG + GROUPS * (NT - 2)
STEPS = UNITS + PV_LAG
G_STEP = 2 * GROUPS - 2

W_UP, W_H1 = 0, 2 * NF * HID
W_H2 = W_H1 + NH * HID
W_DN = W_H2 + NH * HID
W_COLS = W_DN + NH * EMB
CHUNK = 2048
CHUNKS = W_COLS // CHUNK
EARLY_CHUNKS = 2
LATE_CHECK = 8

STATS_TILE, APPLY_TILE, LN1_TILE, QK_TILE = 0, 2, 5, 6
SPLIT_TILES = (8, 9, 11, 12)

HALF = SEQ // 2
GATED = 2 * NH
DEEP = 2 * NH
FFN_TILES = GATED + DEEP
HALVES = 2 * UNITS
B6_USES = 1 + 2 * NT
DOWN_BANKS = (3, 6, 3, 6)
B6_PROJECTED = (2, 4, 6, 8)


def tile_at(n, lag):
    i, rest = divmod(n - lag, GROUPS)
    return i if rest == 0 and 0 <= i < NT else None


def layer_kernel(nc, x, qkvT, outT, ffn_w, ffn_s, s3row, rope, mask, small, out):
    x_v = x.rearrange("b (t p) e -> b p t e", p=P)
    out_v = out.rearrange("b (t p) e -> b t p e", p=P)
    qk_scratch = [nc.dram_tensor(f"qk_scratch{f}", (2, PAIRS // NF, P, SEQ), F32, kind="Internal").ap()
                  for f in range(NF)]
    w_scratch = nc.dram_tensor("w_scratch", (P, W_COLS), F32, kind="Internal").ap()

    ctx = ExitStack()
    with ctx:
        def sem(name):
            return ctx.enter_context(nc.semaphore(name))

        base = (nc.sbuf_base + 31) // 32 * 32
        arena_bytes = (nc.sbuf_usable_end - base) // 32 * 32 - 64
        ctx.enter_context(nc.sbuf_tensor("arena", [P, arena_bytes // 4], F32))
        used = [base]

        def sb(name, shape, dt=F32, at=None):
            size = 4
            for n in shape[1:]:
                size *= n
            if at is None:
                at = used[0]
                used[0] = (at + size + 31) // 32 * 32
                assert used[0] <= base + arena_bytes, (name, used[0] - base, arena_bytes)
            return nc.alloc_sbuf_tensor_at(name, shape, dt, offset=at)

        W = sb("W", [P, W_COLS], F32R)
        a_at = used[0]
        a_hi = sb("a_hi", [P, NH, SEQ], F32R)
        a_lo = sb("a_lo", [P, NH, SEQ], F32R)
        b_at = used[0]
        b_hi = sb("b_hi", [P, NH, SEQ], F32R)
        b_lo = sb("b_lo", [P, NH, SEQ], F32R)
        Sm = sb("Sm", [P, SM_RING, UH, COLS], at=b_at - SM_RING * UH * COLS * 4)
        PgT = sb("PgT", [UH * NGLOB, 2, P], at=b_at - SM_RING * UH * COLS * 4 - 2 * P * 4)
        junk = sb("junk", [P, CHUNK], U16, at=a_at + NH * SEQ * 2)
        inv_sum = sb("inv_sum", [P, EMB], at=a_at + NH * SEQ * 2 + 2 * CHUNK)
        rinv_wide = sb("rinv_wide", [P, HEADS, HD], at=a_at + NH * SEQ * 2 + 2 * CHUNK + EMB * 4)
        assert NH * SEQ * 2 + 2 * CHUNK + 2 * EMB * 4 + 2 * P * 4 + SM_RING * UH * COLS * 4 <= b_at - a_at
        Ks = sb("Ks", [P, PAIRS, SEQ], F32R, at=b_at)
        Qs = sb("Qs", [P, PAIRS, 2, P], F32R, at=b_at + PAIRS * SEQ * 4)
        PT = sb("PT", [P, 2, 2, UH, P], at=b_at + PAIRS * (SEQ + 2 * P) * 4)
        split_at = used[0]
        x2_hi = sb("x2_hi", [P, NF, SEQ], F32R)
        x2_lo = sb("x2_lo", [P, NF, SEQ], F32R)
        split = sb("split", [P, 4, SEQ], F32R, at=split_at)
        Sm0 = sb("Sm0", [P, GROUPS, UH, P], at=split_at)
        x_in = sb("x_in", [P, NT, EMB])
        x_res = sb("x_res", [P, NT, EMB])
        featT = sb("featT", [P, NF, SEQ])
        q = sb("q", [P, NF, SEQ])
        k_at = used[0]
        k = sb("k", [P, NF, SEQ])
        v_even = sb("v_even", [P, NT, EMB])
        v_odd = sb("v_odd", [P, NT, EMB], at=k_at)
        xn = sb("xn", [P, NT, EMB])
        rot = xn[:, :, :].rearrange("p (r t) e -> p r (t e)", r=2)
        silu = xn
        Vg = sb("Vg", [UH * NGLOB, 2, EMB])
        Kg = sb("Kg", [P, NF, HPT, NGLOB])
        Pg = sb("Pg", [P, SM_RING, UH * NGLOB])
        Gs = sb("Gs", [P, 2, HEADS, NGLOB])
        gmin = sb("gmin", [P, 2, HEADS])
        smin = sb("smin", [P, STAT_RING, UH])
        rowsum = sb("rowsum", [P, 2, HEADS])
        rinv = sb("rinv", [P, HEADS])
        bn1 = sb("bn1", [P, NT, 6])
        mv1 = sb("mv1", [P, NT, 2])
        ve1 = sb("ve1", [P, NT])
        rstd1 = sb("rstd1", [P, NT])
        bn2 = sb("bn2", [P, NT, 6])
        mv2 = sb("mv2", [P, NT, 2])
        ve2 = sb("ve2", [P, NT])
        rstd2 = sb("rstd2", [P, NT])
        low_sum = sb("low_sum", [P, CHUNKS])
        low_all = sb("low_all", [P, 1])
        low_int = sb("low_int", [1, 1], I32)
        qkv_w = sb("qkv_w", [P, NF, 3 * EMB])
        out_w = sb("out_w", [P, NF, EMB])
        scales = sb("scales", [P, 4, NH])
        s3 = sb("s3", [P, EMB])
        cos_sin = sb("cos_sin", [P, 2, SEQ])
        msk = sb("msk", [P, 2, KEYS])
        consts = sb("consts", [P, small.shape[1]])
        at = 0
        ident = consts[:, at:at + P]
        at += P
        headmask = consts[:, at:at + HPT]
        at += HPT
        minus_half = consts[:, at:at + 1]
        at += 1
        pick_glob = consts[:, at:at + UH * NGLOB]
        at += UH * NGLOB
        vg_mask = consts[0:UH * NGLOB, at:at + 4 * UH].rearrange("p (u c) -> p u c", u=2)
        at += 4 * UH
        assert at == small.shape[1]

        def unit_scores(n, lo=0, hi=KEYS):
            return Sm[:, n % SM_RING, :, lo:hi] if n >= GROUPS else Sm0[:, n, :, lo - P:hi - P]

        bank = [ctx.enter_context(nc.psum_tensor(f"bank{i}", [P, 512], F32)) for i in range(8)]

        consts_loaded = sem("consts_loaded")
        qkv_loaded = sem("qkv_loaded")
        attn_loaded = sem("attn_loaded")
        scratch_written = [sem(f"scratch_written{n}") for n in range(CHUNKS)]
        w_loaded = [sem(f"w_loaded{n}") for n in range(CHUNKS)]
        x_loaded = sem("x_loaded")
        y_stored = sem("y_stored")
        low_added = sem("low_added")
        low_summed = sem("low_summed")
        low_found = sem("low_found")
        low_ready = sem("low_ready")
        bn1_done = sem("bn1_done")
        mv1_done = sem("mv1_done")
        ve1_done = sem("ve1_done")
        rstd1_done = sem("rstd1_done")
        xn1_done = sem("xn1_done")
        ln1_turned = sem("ln1_turned")
        xnT_done = sem("xnT_done")
        qk_done = sem("qk_done")
        rot_done = sem("rot_done")
        cos_done = sem("cos_done")
        sin_done = sem("sin_done")
        rope_done = sem("rope_done")
        v_done = sem("v_done")
        v_kept = sem("v_kept")
        v_zeroed = sem("v_zeroed")
        v_set = sem("v_set")
        vg_done = sem("vg_done")
        vg_kept = sem("vg_kept")
        down_done = sem("down_done")
        down_scaled = sem("down_scaled")
        y_done = sem("y_done")
        qkhi_done = sem("qkhi_done")
        split_done = sem("split_done")
        split_saved = [[sem(f"split_saved{f}{kind}") for kind in "qk"] for f in range(NF)]
        stacked = [sem(f"stacked{t}") for t in range(NT)]
        kg_done = sem("kg_done")
        g_done = sem("g_done")
        gs_done = sem("gs_done")
        gs_placed = sem("gs_placed")
        b6_free = sem("b6_free")
        s_done = sem("s_done")
        s_free = sem("s_free")
        exp_done = sem("exp_done")
        rinv_spread = sem("rinv_spread")
        rinv_done = sem("rinv_done")
        inv_done = sem("inv_done")
        pg_done = sem("pg_done")
        cur_turned = sem("cur_turned")
        prev_turned = sem("prev_turned")
        glob_turned = sem("glob_turned")
        cur_kept = sem("cur_kept")
        prev_kept = sem("prev_kept")
        glob_kept = sem("glob_kept")
        pv_done = sem("pv_done")
        pv_kept = sem("pv_kept")
        o_done = sem("o_done")
        x1_done = sem("x1_done")
        mv2_done = sem("mv2_done")
        ve2_done = sem("ve2_done")
        rstd2_done = sem("rstd2_done")
        xn2_done = sem("xn2_done")
        ln2_turned = sem("ln2_turned")
        x2hi_done = sem("x2hi_done")
        gated_done = sem("gated_done")
        silu_done = sem("silu_done")
        mul_done = sem("mul_done")
        uphi_done = sem("uphi_done")
        deep_done = sem("deep_done")
        gelu_done = sem("gelu_done")
        ffn_free = sem("ffn_free")

        def at_round(b, per, n):
            return b * per + n

        block = ctx.enter_context(nc.Block())

        N_CONST = 5

        @block.sync
        def _(sp):
            def load_x(b):
                sp.dma_start(x_in[:, :, :], x_v[b]).then_inc(x_loaded, 16)

            def store_y(b):
                for t in range(NT):
                    sp.wait_ge(y_done, at_round(b, NT, t + 1))
                    sp.dma_start(out_v[b, t], x_res[:, t, :]).then_inc(y_stored, 16)

            def next_x(b):
                sp.wait_ge(x1_done, at_round(b, NT, NT))
                load_x(b + 1)

            def save_split(b, f, kind):
                sp.wait_ge(split_done, at_round(b, 2 * NF, 2 * f + kind + 1))
                sp.nop(nofuse=True)
                if f == 0 and kind == 0 and not (isinstance(b, int) and b == 0):
                    for t in range(NT):
                        sp.wait_ge(stacked[t], at_round(b, 16 * LOADS, 0))
                        sp.nop(nofuse=True)
                rows = qk_scratch[f][kind].rearrange("s (e a d) c -> a s e d c", e=2, a=PARTS)
                for part, source in enumerate((Q_PARTS, K_PARTS)[kind]):
                    sp.dma_start(rows[part].rearrange("s e d c -> (s e) d c"),
                                 split[:, source, :].bitcast(F32)).then_inc(split_saved[f][kind], 16)

            def prepare(b):
                for f in range(NF):
                    for kind in range(2):
                        save_split(b, f, kind)

            def load_stacks(b, t):
                if t == 0:
                    for saved in (saved for kinds in split_saved for saved in kinds):
                        sp.wait_ge(saved, at_round(b, 16 * SAVES, 16 * SAVES))
                        sp.nop(nofuse=True)
                    if not (isinstance(b, int) and b == 0):
                        sp.wait_ge(deep_done, at_round(b, DEEP, 0))
                        sp.nop(nofuse=True)
                if t >= 2:
                    sp.wait_ge(s_done, at_round(b, HALVES, 2 * GROUPS * (t - 1)))
                    sp.nop(nofuse=True)
                cols = slice(t * P, (t + 1) * P)
                for f in range(NF):
                    pairs = slice(f * PAIRS // NF, (f + 1) * PAIRS // NF)
                    for kind, dst in enumerate((Qs[:, pairs, t % 2, :], Ks[:, pairs, cols])):
                        sp.dma_start(dst.bitcast(F32), qk_scratch[f][kind].rearrange("s p c -> p s c")[:, :, cols])\
                            .then_inc(stacked[t], 16)

            load_x(0)
            sp.dma_start(consts[:, :], small).then_inc(consts_loaded, 16)
            sp.dma_start(qkv_w[:, :, :], qkvT).then_inc(qkv_loaded, 16)
            sp.dma_start(cos_sin[:, :, :], rope).then_inc(attn_loaded, 16)
            sp.dma_start(msk[:, :, :], mask).then_inc(attn_loaded, 16)
            sp.dma_start(out_w[:, :, :], outT).then_inc(attn_loaded, 16)
            sp.dma_start(scales[:, :, :], ffn_s).then_inc(attn_loaded, 16)
            sp.dma_start(s3[:, :], s3row.broadcast_to([P, EMB])).then_inc(attn_loaded, 16)
            def save_weights(n):
                cols = slice(n * CHUNK, (n + 1) * CHUNK)
                sp.dma_start(w_scratch[:, cols], ffn_w[:, cols]).then_inc(scratch_written[n], 16)

            def load_weights(n):
                cols = slice(n * CHUNK, (n + 1) * CHUNK)
                sp.wait_ge(scratch_written[n], 16)
                sp.dma_start(W[:, cols].bitcast(F32), w_scratch[:, cols]).then_inc(w_loaded[n], 16)

            for n in range(EARLY_CHUNKS):
                save_weights(n)
            for n in range(EARLY_CHUNKS):
                load_weights(n)
            prepare(0)
            load_stacks(0, 0)
            load_stacks(0, 1)
            save_weights(2)
            save_weights(3)
            load_weights(2)
            load_weights(3)
            load_stacks(0, 2)
            save_weights(4)
            save_weights(5)
            load_weights(4)
            load_stacks(0, 3)
            save_weights(6)
            for n in range(5, CHUNKS):
                if n + 2 < CHUNKS:
                    save_weights(n + 2)
                load_weights(n)

            def one_round(b):
                load_stacks(b, 0)
                load_stacks(b, 1)
                store_y(b - 1)
                load_stacks(b, 2)
                load_stacks(b, 3)

            next_x(0)
            prepare(1)
            with sp.Fori(1, NB - 1) as b:
                one_round(b)
                next_x(b)
                prepare(b + 1)
            one_round(NB - 1)
            store_y(NB - 1)
            sp.wait_ge(y_stored, 16 * NT * NB)

        @block.tensor
        def _(pe):
            def ln1_transposes(b):
                for t in range(NT):
                    pe.wait_ge(xn1_done, at_round(b, NT, t + 1))
                    for f in range(NF):
                        mm = nc.tensor.transpose(bank[4 + f][:, t * P:(t + 1) * P],
                                                 xn[:, t, f * P:(f + 1) * P], ident)
                        if t == NT - 1:
                            mm.then_inc(ln1_turned, 1)

            def qk_projection(b):
                pe.wait_ge(xnT_done, at_round(b, NF, NF))
                for n in range(2 * NF):
                    f, kind = n // 2, n % 2
                    col = kind * EMB + f * P
                    for kk in range(NF):
                        mm = nc.tensor.matmul(bank[[6, 7, 4, 5][n]][:, :], qkv_w[:, kk, col:col + P],
                                              featT[:, kk, :], start=(kk == 0), stop=(kk == NF - 1))
                    mm.then_inc(qk_done, 1)

            def v_projection(b):
                for t in range(NT):
                    pe.wait_ge(rot_done, at_round(b, 2 * NF, t + 1))
                    for kk in range(NF):
                        mm = nc.tensor.matmul(bank[[6, 7, 4, 5][t]][:, 0:EMB], featT[:, kk, t * P:(t + 1) * P],
                                              qkv_w[:, kk, 2 * EMB:3 * EMB], start=(kk == 0), stop=(kk == NF - 1))
                    mm.then_inc(v_done, 1)
                pe.wait_ge(v_kept, at_round(b, 2 * NT, 2))
                pe.wait_ge(v_set, 1)
                for part, v in enumerate((v_even, v_odd)):
                    mm = nc.tensor.matmul(bank[6][0:UH * NGLOB, 0:EMB], pick_glob, v[:, 0, :],
                                          start=(part == 0), stop=(part == 1))
                mm.then_inc(vg_done, 1)

            def down_tile(b, t, general):
                if t == 0:
                    pe.wait_ge(ffn_free, at_round(b, FFN_TILES, FFN_TILES))
                elif t >= 2:
                    pe.wait_ge(y_done, at_round(b, NT, t - 1))
                for kk in range(NH):
                    for part, h in enumerate((a_hi, a_lo)):
                        lhsT = h[:, kk, t * P:(t + 1) * P]
                        rhs = W[:, W_DN + kk * EMB:W_DN + (kk + 1) * EMB]
                        if general:
                            lhsT, rhs = lhsT.bitcast(F32), rhs.bitcast(F32)
                        mm = nc.tensor.matmul(bank[DOWN_BANKS[t]][:, 0:EMB], lhsT, rhs,
                                              start=(kk == 0 and part == 0), stop=(kk == NH - 1 and part == 1))
                mm.then_inc(down_done, 1)

            def out_projection(b, i):
                pe.wait_ge(b6_free, at_round(b, B6_USES, B6_PROJECTED[i] - 1))
                pe.wait_ge(pv_kept, at_round(b, NT, i + 1))
                for f in range(NF):
                    mm = nc.tensor.matmul(bank[6][:, 0:EMB], featT[:, f, i * P:(i + 1) * P], out_w[:, f, :],
                                          start=(f == 0), stop=(f == NF - 1))
                mm.then_inc(o_done, 1)

            def ln2_transposes(b, i):
                pe.wait_ge(b6_free, at_round(b, B6_USES, B6_PROJECTED[i]))
                pe.wait_ge(xn2_done, at_round(b, NT, i + 1))
                for f in range(NF):
                    mm = nc.tensor.transpose(bank[6][:, f * P:(f + 1) * P], xn[:, i, f * P:(f + 1) * P], ident)
                mm.then_inc(ln2_turned, 1)

            def attention(b, first, general=None):

                def global_scores():
                    pe.wait_ge(kg_done, at_round(b, 1, 1))
                    pe.wait_ge(vg_kept, at_round(b, 2, 2))
                    if not first:
                        pe.wait_ge(y_done, at_round(b, NT, 0))
                    for i in range(2):
                        for f in range(NF):
                            col = (i * NF + f) * HPT * NGLOB
                            mm = nc.tensor.matmul(bank[6][:, col:col + HPT * NGLOB],
                                                  q[:, f, (i + 2) * P:(i + 3) * P],
                                                  Kg[:, f, :, :].rearrange("p h j -> p (h j)"), start=True, stop=True)
                    mm.then_inc(g_done, 1)

                def scores(n):
                    i, g = n // GROUPS, n % GROUPS
                    if g == 0:
                        pe.wait_ge(stacked[i], at_round(b, 16 * LOADS, 16 * LOADS))
                    lo = 0 if i else P
                    for half in range(2):
                        hs = 2 * n + half
                        if hs >= 3:
                            pe.wait_ge(s_free, at_round(b, HALVES, hs - 2))
                        for c2 in range(2):
                            rows = slice(half * PARTS * HD, (half + 1) * PARTS * HD)
                            pair = g * UH // 2 + c2
                            mm = nc.tensor.matmul(bank[hs % 3][:, c2 * KEYS + lo:(c2 + 1) * KEYS],
                                                  Qs[rows, pair, i % 2, :],
                                                  Ks[rows, pair, i * P + lo - P:(i + 1) * P], start=True, stop=True)
                        mm.then_inc(s_done, 1)

                def transposes(n):
                    i = n // GROUPS
                    pe.wait_ge(exp_done, at_round(b, UNITS, n + 1))
                    if n:
                        pe.wait_ge(cur_kept, at_round(b, UNITS, n))
                    else:
                        pe.wait_ge(v_kept, at_round(b, 2 * NT, 2 * NT))
                    for c in range(UH):
                        mm = nc.tensor.transpose(bank[5][:, c * P:(c + 1) * P], unit_scores(n, P)[:, c, :], ident)
                    mm.then_inc(cur_turned, 1)
                    if i == 0:
                        return
                    m = n - GROUPS
                    if m:
                        pe.wait_ge(prev_kept, at_round(b, LATER, m))
                    for c in range(UH):
                        mm = nc.tensor.transpose(bank[4][:, c * P:(c + 1) * P], Sm[:, n % SM_RING, c, 0:P], ident)
                    mm.then_inc(prev_turned, 1)
                    if i == 1:
                        return
                    m = n - 2 * GROUPS
                    if m:
                        pe.wait_ge(glob_kept, at_round(b, FAR, m))
                    pe.wait_ge(pg_done, at_round(b, FAR, m + 1))
                    nc.tensor.transpose(bank[3][0:UH * NGLOB, 0:P], Pg[:, n % SM_RING, :], ident)\
                        .then_inc(glob_turned, 1)

                def weighted_values(n):
                    i, g = n // GROUPS, n % GROUPS
                    f = g * UH // HPT
                    pe.wait_ge(cur_kept, at_round(b, UNITS, n + 1))
                    if i:
                        pe.wait_ge(prev_kept, at_round(b, LATER, n - GROUPS + 1))
                        if i > 1:
                            pe.wait_ge(glob_kept, at_round(b, FAR, n - 2 * GROUPS + 1))
                        if g == 0:
                            pe.wait_ge(pv_kept, at_round(b, NT, i))
                    out = bank[7][:, f * P:(f + 1) * P]
                    v = (v_even, v_odd)[g % 2]
                    for side in ((1, 0) if i else (1,)):
                        for c in range(UH):
                            col = f * P + 32 * c
                            mm = nc.tensor.matmul(out[32 * c:32 * c + 32, :], v[:, i - 1 + side, col:col + 32],
                                                  PT[:, n % 2, side, c, :], start=(g % 2 == 0 and side == 1),
                                                  stop=(g % 2 == 1 and side == (0 if i == 1 else 1) and i < 2),
                                                  skip_group_check=True)
                    if i > 1:
                        mm = nc.tensor.matmul(out, Vg[:, g % 2, f * P:(f + 1) * P], PgT[:, n % 2, :],
                                              start=False, stop=(g % 2 == 1), skip_group_check=True)
                    if g == GROUPS - 1:
                        pe.wait_ge(rinv_spread, at_round(b, NT, i + 1))
                        for f in range(NF):
                            mm = nc.tensor.transpose(
                                bank[7][:, EMB + f * P:EMB + (f + 1) * P],
                                rinv_wide[:, f * HPT:(f + 1) * HPT, :].rearrange("p h d -> p (h d)"), ident)
                    mm.then_inc(pv_done, 1)

                def step(n):
                    if n < NT and not first:
                        if n == 1:
                            pe.wait_ge(vg_kept, at_round(b, 2, 2))
                        down_tile(b - 1, n, general)
                    if n < UNITS:
                        scores(n)
                    if 0 <= n - T_LAG < UNITS:
                        transposes(n - T_LAG)
                    if 0 <= n - PV_LAG < UNITS:
                        weighted_values(n - PV_LAG)
                    if (i := tile_at(n, TURN_LAG)) is not None:
                        ln2_transposes(b, i)
                    if n == G_STEP:
                        global_scores()
                    if (i := tile_at(n, O_LAG)) is not None:
                        out_projection(b, i)

                return step

            def ffn_tile(out, w_at, width, m, h_hi, h_lo, tiles, general, wait=None):
                for kk in range(tiles):
                    if wait is not None:
                        wait(kk)
                    lhsT = W[:, w_at + kk * width + m * P:w_at + kk * width + (m + 1) * P]
                    if general:
                        lhsT = lhsT.bitcast(F32)
                    for part, h in enumerate((h_hi, h_lo)):
                        rhs = h[:, kk, :].bitcast(F32) if general else h[:, kk, :]
                        mm = nc.tensor.matmul(out, lhsT, rhs, start=(kk == 0 and part == 0),
                                              stop=(kk == tiles - 1 and part == 1))
                return mm

            def gated_tile(b, s, general):
                half, m = s // NH, s % NH
                if s == 0:
                    pe.wait_ge(s_free, at_round(b, HALVES, HALVES))
                if s == 3:
                    pe.wait_ge(glob_kept, at_round(b, FAR, FAR))
                if m == 0:
                    pe.wait_ge(x2hi_done, at_round(b, NT, NT // 2 * (half + 1)))
                    pe.wait_ge(b6_free, at_round(b, B6_USES, B6_PROJECTED[NT // 2 * (half + 1) - 1] + 1))
                if s >= 4:
                    pe.wait_ge(ffn_free, at_round(b, FFN_TILES, s - 3))
                for u in range(2):
                    mm = ffn_tile(bank[s % 4][:, u * HALF:(u + 1) * HALF], W_UP + u * NF * HID, HID, m,
                                  x2_hi[:, :, half * HALF:(half + 1) * HALF],
                                  x2_lo[:, :, half * HALF:(half + 1) * HALF], NF, general)
                mm.then_inc(gated_done, 1)

            def ffn_hidden(b, general, last, step):
                between = {1: lambda: step and step(STEPS - 2),
                           2: lambda: (ln2_transposes(b, NT - 2), step and step(STEPS - 1)),
                           3: lambda: out_projection(b, NT - 1), 7: lambda: ln2_transposes(b, NT - 1)}
                for s in range(GATED):
                    if s in between:
                        between[s]()
                    gated_tile(b, s, general)
                for layer, (w_at, h_hi, h_lo) in enumerate(((W_H1, a_hi, a_lo), (W_H2, b_hi, b_lo))):
                    for m in range(NH):
                        before = GATED + NH * layer
                        pe.wait_ge(ffn_free, at_round(b, FFN_TILES, before + m - 3))
                        n = layer * NH + m
                        if n == LN1_TILE and not last:
                            ln1_transposes(b + 1)
                        if n == QK_TILE and not last:
                            qk_projection(b + 1)
                        wait = None
                        if m == 0:
                            def wait(kk, before=before):
                                if kk >= NH - 4:
                                    pe.wait_ge(ffn_free, at_round(b, FFN_TILES, before - NH + kk + 1))
                        ffn_tile(bank[m % 4][:, :], w_at, HID, m, h_hi, h_lo, NH, general, wait)\
                            .then_inc(deep_done, 1)
                if not last:
                    v_projection(b + 1)

            pe.wait_ge(consts_loaded, 16)
            ln1_transposes(0)
            pe.wait_ge(qkv_loaded, 16)
            qk_projection(0)
            pe.wait_ge(attn_loaded, 16 * N_CONST)
            v_projection(0)
            step = attention(0, True)
            for n in range(STEPS):
                step(n)
            pe.wait_ge(low_found, 1)
            pe.wait_ge(s_free, HALVES)
            nc.tensor.matmul(bank[0][0:1, 0:1], low_all[:, :], minus_half, start=True, stop=True)\
                .then_inc(low_added, 1)
            pe.wait_ge(low_ready, 1)
            low_bits = pe.value_load(low_int[0:1, 0:1], min_val=0, max_val=1)

            def rounds(general):
                def one_round(b, last=False):
                    step = attention(b, False, general)
                    for n in range(STEPS - 2):
                        step(n)
                    ffn_hidden(b, general, last, step)

                ffn_hidden(0, general, False, None)
                with pe.Fori(1, NB - 1) as b:
                    one_round(b)
                one_round(NB - 1, last=True)
                for t in range(NT):
                    down_tile(NB - 1, t, general)

            with pe.If(low_bits):
                rounds(True)
            with pe.Else():
                rounds(False)

        @block.scalar
        def _(act):
            def keep_xnT(b):
                for f in range(NF):
                    act.wait_ge(ln1_turned, at_round(b, NF, f + 1))
                    nc.scalar.copy(featT[:, f, :], bank[4 + f][:, :]).then_inc(xnT_done, 1)

            def split_hi(b, n):
                f, kind = n // 2, n % 2
                act.wait_ge(rope_done, at_round(b, 2 * NF, n + 1))
                if f:
                    act.wait_ge(split_saved[0][kind], at_round(b, 16 * SAVES, 16 * SAVES))
                elif not (isinstance(b, int) and b == 0):
                    act.wait_ge(split_saved[1][kind], at_round(b, 16 * SAVES, 0))
                nc.scalar.activation(split[:, 2 * kind, :], (q, k)[kind][:, f, :], ACT.Copy,
                                     scale=SPLIT_SCALE[kind]).then_inc(qkhi_done, 1)

            def keep_v(b):
                for t in range(NT):
                    act.wait_ge(v_done, at_round(b, NT, t + 1))
                    if t == 0:
                        act.wait_ge(v_zeroed, b + 1)
                    for unit, v in enumerate((v_even, v_odd)):
                        half = lambda tile: tile.rearrange("p (c u d) -> p c u d", u=2, d=HD)[:, :, unit, :]
                        nc.scalar.copy(half(v[:, t, :]), half(bank[[6, 7, 4, 5][t]][:, 0:EMB])).then_inc(v_kept, 1)

            def keep_x2hi(b, i):
                act.wait_ge(ln2_turned, at_round(b, NT, i + 1))
                if i == 0:
                    for saved in split_saved[1]:
                        act.wait_ge(saved, at_round(b, 16 * SAVES, 16 * SAVES))
                nc.scalar.copy(x2_hi[:, :, i * P:(i + 1) * P],
                               bank[6][:, 0:EMB].rearrange("p (f q) -> p f q", f=NF)).then_inc(x2hi_done, 1)

            def attention(b, first):
                def exponentials(n):
                    i, g, r = n // GROUPS, n % GROUPS, n % STAT_RING
                    c0, c1 = (0 if i else P), (COLS if i > 1 else KEYS)
                    act.wait_ge(s_free, at_round(b, HALVES, 2 * n + 2))
                    if i > 1:
                        act.wait_ge(gs_placed, at_round(b, FAR, n - 2 * GROUPS + 1))
                    if i > 1 and g == 0:
                        act.wait_ge(rinv_done, at_round(b, NT, i - 1))
                    for c in range(UH):
                        if c == UH // 2 and (t := tile_at(n, SPLIT_LAG)) is not None:
                            keep_x2hi(b, t)
                        row = unit_scores(n, c0, c1)[:, c, :]
                        col = g // 2 * HPT + 2 * c + g % 2
                        ex = nc.scalar.activation(row, row, ACT.Exp, bias=smin[:, r, c:c + 1], scale=-1.0,
                                                  accum_out=rowsum[:, i % 2, col:col + 1])
                    ex.then_inc(exp_done, 1)

                def keep_prev(n):
                    act.wait_ge(prev_turned, at_round(b, LATER, n - GROUPS + 1))
                    act.wait_ge(pv_done, at_round(b, UNITS, n - 1))
                    nc.scalar.copy(PT[:, n % 2, 0, :, :].rearrange("p c q -> p (c q)"), bank[4][:, :])\
                        .then_inc(prev_kept, 1)
                    if n >= 2 * GROUPS:
                        act.wait_ge(glob_turned, at_round(b, FAR, n - 2 * GROUPS + 1))
                        nc.scalar.copy(PgT[:, n % 2, :], bank[3][0:UH * NGLOB, 0:P]).then_inc(glob_kept, 1)

                for n in range(STEPS):
                    if GROUPS <= n - T_LAG < UNITS:
                        keep_prev(n - T_LAG)
                    if n < UNITS:
                        exponentials(n)
                    if first and EARLY_CHUNKS <= n - LATE_CHECK < CHUNKS:
                        check_weights(n - LATE_CHECK)

            def check_weights(n):
                act.wait_ge(w_loaded[n], 16)
                if n:
                    act.wait_ge(low_summed, n)
                low_halves = W[:, n * CHUNK:(n + 1) * CHUNK].bitcast(U16)[:, 0:2 * CHUNK:2]
                nc.scalar.activation(junk[:, :], low_halves, ACT.Copy, accum_out=low_sum[:, n:n + 1]).then_inc(low_summed, 1)

            def ffn_hidden(b, last):
                def up_hi(s):
                    half, m = s // NH, s % NH
                    act.wait_ge(mul_done, at_round(b, GATED, s + 1))
                    nc.scalar.copy(a_hi[:, m, half * HALF:(half + 1) * HALF], bank[s % 4][:, HALF:SEQ])\
                        .then_inc(uphi_done, 1)

                for s in range(GATED):
                    act.wait_ge(gated_done, at_round(b, GATED, s + 1))
                    if s >= 2:
                        act.wait_ge(mul_done, at_round(b, GATED, s - 1))
                    nc.scalar.activation(silu[:, s % 2, :], bank[s % 4][:, 0:HALF], ACT.Silu,
                                         scale=scales[:, 0, s % NH:s % NH + 1]).then_inc(silu_done, 1)
                    if s:
                        up_hi(s - 1)
                    if s == 0:
                        keep_x2hi(b, NT - 2)
                    if s == 6:
                        keep_x2hi(b, NT - 1)
                up_hi(GATED - 1)
                for n in range(DEEP):
                    layer, m = n // NH, n % NH
                    h_hi = (b_hi, a_hi)[layer]
                    ps = bank[m % 4][:, :]
                    s = scales[:, 2 + layer, m:m + 1]
                    if n == LN1_TILE and not last:
                        keep_xnT(b + 1)
                    act.wait_ge(deep_done, at_round(b, DEEP, n + 1))
                    nc.scalar.activation(h_hi[:, m, :], ps, ACT.Gelu, scale=s)
                    nc.scalar.activation(ps, ps, ACT.Gelu, scale=s).then_inc(gelu_done, 1)
                    if n in SPLIT_TILES and not last:
                        split_hi(b + 1, SPLIT_TILES.index(n))
                if not last:
                    keep_v(b + 1)

            keep_xnT(0)
            for n in range(2 * NF):
                split_hi(0, n)
            keep_v(0)
            for n in range(EARLY_CHUNKS):
                check_weights(n)
            act.wait_ge(attn_loaded, 16 * N_CONST)
            attention(0, True)
            ffn_hidden(0, False)
            with act.Fori(1, NB - 1) as b:
                attention(b, False)
                ffn_hidden(b, False)
            attention(NB - 1, False)
            ffn_hidden(NB - 1, True)

        @block.vector
        def _(dve):
            def ln1_stats(b, t):
                if t == 0:
                    dve.wait_ge(x_loaded, at_round(b, 16, 16))
                nc.vector.bn_stats(bn1[:, t, :], x_in[:, t, :]).then_inc(bn1_done, 1)
                dve.wait_ge(bn1_done, at_round(b, NT, t + 1))
                dve.nop(nofuse=True)
                nc.vector.bn_aggr(mv1[:, t, :], bn1[:, t, :]).then_inc(mv1_done, 1)

            def ln1_apply(b, t):
                dve.wait_ge(rstd1_done, at_round(b, NT, t + 1))
                nc.vector.tensor_scalar(xn[:, t, :], x_in[:, t, :], mv1[:, t, 0:1], rstd1[:, t:t + 1],
                                        ALU.subtract, ALU.mult).then_inc(xn1_done, 1)

            def rope(b, n):
                src = bank[[6, 7, 4, 5][n]]
                dst = (q, k)[n % 2][:, n // 2, :]
                dve.wait_ge(qk_done, at_round(b, 2 * NF, n + 1))
                if n >= 2:
                    dve.wait_ge(rope_done, at_round(b, 2 * NF, n - 1))
                nc.vector.tensor_tensor(dst, src[:, :], cos_sin[:, 0, :], ALU.mult).then_inc(cos_done, 1)
                nc.vector.stream_shuffle(rot[:, n % 2, :], src[:, :], [p ^ 1 for p in range(32)])\
                    .then_inc(rot_done, 1)

            def split_lo(b, n):
                f, kind = n // 2, n % 2
                dve.wait_ge(qkhi_done, at_round(b, 2 * NF, n + 1))
                nc.vector.scalar_tensor_tensor(split[:, 2 * kind + 1, :], (q, k)[kind][:, f, :], SPLIT_SCALE[kind],
                                               split[:, 2 * kind, :].bitcast(F32), ALU.mult, ALU.subtract)\
                    .then_inc(split_done, 1)

            def keep_vg(b):
                dve.wait_ge(vg_done, at_round(b, 1, 1))
                for unit in range(2):
                    nc.vector.tensor_tensor(
                        Vg[:, unit, :].rearrange("p (f c d) -> p f c d", f=NF, d=HD),
                        bank[6][0:UH * NGLOB, 0:EMB].rearrange("p (f c d) -> p f c d", f=NF, d=HD),
                        vg_mask[:, unit, :].unsqueeze(1).unsqueeze(3).broadcast_to([UH * NGLOB, NF, 2 * UH, HD]),
                        ALU.mult).then_inc(vg_kept, 1)

            def global_keys(b):
                dve.wait_ge(rope_done, at_round(b, 2 * NF, 2 * NF))
                nc.vector.tensor_tensor(
                    Kg[:, :, :, :], k[:, :, 0:NGLOB].unsqueeze(2).broadcast_to([P, NF, HPT, NGLOB]),
                    headmask.unsqueeze(1).unsqueeze(3).broadcast_to([P, NF, HPT, NGLOB]), ALU.mult).then_inc(kg_done, 1)

            def finish_y(b, t):
                ps = bank[DOWN_BANKS[t]][:, 0:EMB]
                dve.wait_ge(down_done, at_round(b, NT, t + 1))
                nc.vector.tensor_tensor(ps, ps, s3[:, :], ALU.mult).then_inc(down_scaled, 1)
                dve.wait_ge(down_scaled, at_round(b, NT, t + 1))
                nc.vector.tensor_tensor(x_res[:, t, :], x_res[:, t, :], ps, ALU.add).then_inc(y_done, 1)

            def keep_heads(b, i):
                dve.wait_ge(pv_done, at_round(b, UNITS, GROUPS * (i + 1)))
                nc.vector.tensor_copy(inv_sum[:, :], bank[7][:, EMB:2 * EMB]).then_inc(inv_done, 1)
                dve.wait_ge(inv_done, at_round(b, NT, i + 1))
                nc.vector.tensor_tensor(featT[:, :, i * P:(i + 1) * P],
                                        bank[7][:, 0:EMB].rearrange("p (f q) -> p f q", f=NF),
                                        inv_sum[:, :].rearrange("p (f q) -> p f q", f=NF), ALU.mult)\
                    .then_inc(pv_kept, 1)

            def residual(b, i):
                dve.wait_ge(o_done, at_round(b, NT, i + 1))
                if i == 0 and not (isinstance(b, int) and b == 0):
                    dve.wait_ge(y_stored, at_round(b, 16 * NT, 0))
                nc.vector.tensor_tensor(x_res[:, i, :], x_in[:, i, :], bank[6][:, 0:EMB], ALU.add)\
                    .then_inc(b6_free, 1)

            def ln2_stats(b, i):
                dve.wait_ge(b6_free, at_round(b, B6_USES, B6_PROJECTED[i]))
                nc.vector.bn_stats(bn2[:, i, :], x_res[:, i, :]).then_inc(x1_done, 1)

            def ln2_moments(b, i):
                dve.wait_ge(x1_done, at_round(b, NT, i + 1))
                dve.nop(nofuse=True)
                nc.vector.bn_aggr(mv2[:, i, :], bn2[:, i, :]).then_inc(mv2_done, 1)

            def ln2_apply(b, i):
                dve.wait_ge(rstd2_done, at_round(b, NT, i + 1))
                nc.vector.tensor_scalar(xn[:, i, :], x_res[:, i, :], mv2[:, i, 0:1], rstd2[:, i:i + 1],
                                        ALU.subtract, ALU.mult).then_inc(xn2_done, 1)

            def keep_x2lo(b, i):
                dve.wait_ge(x2hi_done, at_round(b, NT, i + 1))
                nc.vector.tensor_tensor(
                    x2_lo[:, :, i * P:(i + 1) * P], bank[6][:, 0:EMB].rearrange("p (f q) -> p f q", f=NF),
                    x2_hi[:, :, i * P:(i + 1) * P].bitcast(F32), ALU.subtract).then_inc(b6_free, 1)

            def attention(b, first):
                def global_scores():
                    dve.wait_ge(g_done, at_round(b, 1, 1))
                    nc.vector.tensor_copy(Gs[:, :, :, :].rearrange("p i h j -> p (i h j)"),
                                          bank[6][:, 0:2 * HEADS * NGLOB]).then_inc(b6_free, 1)
                    dve.wait_ge(b6_free, at_round(b, B6_USES, 1))
                    nc.vector.tensor_reduce(gmin[:, :, :].rearrange("p i h -> p (i h)"),
                                            Gs[:, :, :, :].rearrange("p i h j -> p (i h) j"),
                                            AX.X, ALU.min).then_inc(gs_done, 1)

                def masked_min(n):
                    i, g, r = n // GROUPS, n % GROUPS, n % STAT_RING
                    lo = 0 if i else P
                    if n >= GROUPS + SM_RING:
                        m = n - SM_RING
                        dve.wait_ge(prev_turned, at_round(b, LATER, m - GROUPS + 1))
                    elif n >= STAT_RING:
                        dve.wait_ge(exp_done, at_round(b, UNITS, n - STAT_RING + 1))
                    if n == 2 * GROUPS:
                        dve.wait_ge(gs_done, at_round(b, 1, 1))
                    for half in range(2):
                        hs = 2 * n + half
                        dve.wait_ge(s_done, at_round(b, HALVES, hs + 1))
                        dve.nop(nofuse=True)
                        for c2 in range(2):
                            c = 2 * c2 + half
                            h = g * UH + c
                            tt = nc.vector.tensor_tensor_reduce(
                                out=unit_scores(n, lo)[:, c, :], in0=bank[hs % 3][:, c2 * KEYS + lo:(c2 + 1) * KEYS],
                                in1=msk[:, int(i == 1), lo:KEYS], scale=1.0,
                                scalar=gmin[:, i - 2, h:h + 1] if i > 1 else FAR_OFF,
                                op0=ALU.add, op1=ALU.min, accum_out=smin[:, r, c:c + 1])
                        tt.then_inc(s_free, 1)

                def inverse_sums(i):
                    dve.wait_ge(exp_done, at_round(b, UNITS, GROUPS * (i + 1)))
                    if i:
                        dve.wait_ge(rinv_spread, at_round(b, NT, i))
                    nc.vector.reciprocal(rinv[:, :], rowsum[:, i % 2, :]).then_inc(rinv_done, 1)

                def keep_cur(n):
                    dve.wait_ge(cur_turned, at_round(b, UNITS, n + 1))
                    if n >= 2:
                        dve.wait_ge(pv_done, at_round(b, UNITS, n - 1))
                    nc.vector.tensor_copy(PT[:, n % 2, 1, :, :].rearrange("p c q -> p (c q)"), bank[5][:, :])\
                        .then_inc(cur_kept, 1)

                for n in range(STEPS):
                    if n < NT and not first:
                        finish_y(b - 1, n)
                    if (i := tile_at(n, HEADS_LAG)) is not None:
                        keep_heads(b, i)
                    if n < UNITS:
                        masked_min(n)
                    if (i := tile_at(n, SPLIT_LAG + 1)) is not None:
                        keep_x2lo(b, i)
                    if n <= LAST_RES and (i := tile_at(n, RES_LAG + 1)) is not None:
                        ln2_moments(b, i)
                    if (i := tile_at(n, SPREAD_LAG)) is not None:
                        inverse_sums(i)
                    if (i := tile_at(n, RES_LAG)) is not None:
                        residual(b, i)
                    if n == LAST_RES:
                        ln2_stats(b, NT - 2)
                        ln2_moments(b, NT - 2)
                    if 0 <= n - T_LAG < UNITS:
                        keep_cur(n - T_LAG)
                    if n < LAST_RES and (i := tile_at(n, RES_LAG)) is not None:
                        ln2_stats(b, i)
                    if n == LAST_RES + 1:
                        ln2_apply(b, NT - 2)
                    if n == G_STEP + 1:
                        global_scores()
                if first:
                    low_bits()

            def low_bits():
                dve.wait_ge(low_summed, CHUNKS)
                nc.vector.tensor_reduce(low_all[:, :], low_sum[:, :], AX.X, ALU.max).then_inc(low_found, 1)
                dve.wait_ge(low_added, 1)
                nc.vector.tensor_scalar(low_int[:, :], bank[0][0:1, 0:1], 0.0, None, ALU.is_lt).then_inc(low_ready, 1)

            def ffn_hidden(b, last):
                def up_lo(s):
                    half, m = s // NH, s % NH
                    cols = slice(half * HALF, (half + 1) * HALF)
                    dve.wait_ge(uphi_done, at_round(b, GATED, s + 1))
                    nc.vector.tensor_tensor(a_lo[:, m, cols], bank[s % 4][:, HALF:SEQ],
                                            a_hi[:, m, cols].bitcast(F32), ALU.subtract).then_inc(ffn_free, 1)

                for s in range(GATED):
                    up = bank[s % 4][:, HALF:SEQ]
                    dve.wait_ge(silu_done, at_round(b, GATED, s + 1))
                    nc.vector.scalar_tensor_tensor(up, up, scales[:, 1, s % NH:s % NH + 1], silu[:, s % 2, :],
                                                   ALU.mult, ALU.mult).then_inc(mul_done, 1)
                    if s:
                        up_lo(s - 1)
                    for at, stage, t in ((0, keep_x2lo, NT - 2), (0, keep_heads, NT - 1), (2, residual, NT - 1),
                                         (2, ln2_stats, NT - 1), (2, ln2_moments, NT - 1),
                                         (3, ln2_apply, NT - 1), (6, keep_x2lo, NT - 1)):
                        if s == at:
                            stage(b, t)
                up_lo(GATED - 1)
                for n in range(DEEP):
                    layer, m = n // NH, n % NH
                    h_hi, h_lo = ((b_hi, b_lo), (a_hi, a_lo))[layer]
                    dve.wait_ge(gelu_done, at_round(b, DEEP, n + 1))
                    nc.vector.tensor_tensor(h_lo[:, m, :], bank[m % 4][:, :], h_hi[:, m, :].bitcast(F32),
                                            ALU.subtract).then_inc(ffn_free, 1)
                    if not last:
                        for t in range(NT):
                            if n == STATS_TILE + t // 2:
                                ln1_stats(b + 1, t)
                            if n == APPLY_TILE + t // 2:
                                ln1_apply(b + 1, t)
                        if QK_TILE <= n < QK_TILE + 2 * NF:
                            rope(b + 1, n - QK_TILE)
                        if n in SPLIT_TILES:
                            split_lo(b + 1, SPLIT_TILES.index(n))
                        if n == SPLIT_TILES[-1]:
                            global_keys(b + 1)
                if not last:
                    keep_vg(b + 1)

            for t in range(NT):
                ln1_stats(0, t)
            for t in range(NT):
                ln1_apply(0, t)
            dve.wait_ge(consts_loaded, 16)
            dve.wait_ge(attn_loaded, 16 * N_CONST)
            for n in range(2 * NF):
                rope(0, n)
            for n in range(2 * NF):
                split_lo(0, n)
            global_keys(0)
            keep_vg(0)
            attention(0, True)
            ffn_hidden(0, False)
            with dve.Fori(1, NB - 1) as b:
                attention(b, False)
                ffn_hidden(b, False)
            attention(NB - 1, False)
            ffn_hidden(NB - 1, True)
            for t in range(NT):
                finish_y(NB - 1, t)

        @block.gpsimd
        def _(pool):
            def rsqrt(b, t, mv, ve, rstd, stats, ve_done, done):
                pool.wait_ge(stats, at_round(b, NT, t + 1))
                pool.nop(nofuse=True)
                nc.gpsimd.tensor_scalar(ve[:, t:t + 1], mv[:, t, 1:2], LN_EPS, None, ALU.add).then_inc(ve_done, 1)
                pool.wait_ge(ve_done, at_round(b, NT, t + 1))
                nc.gpsimd.tensor_tensor(rstd[:, t:t + 1], ve[:, t:t + 1], minus_half, ALU.pow).then_inc(done, 1)

            def ln1(b):
                for t in range(NT):
                    rsqrt(b, t, mv1, ve1, rstd1, mv1_done, ve1_done, rstd1_done)

            def rope(b):
                for n in range(2 * NF):
                    dst = (q, k)[n % 2][:, n // 2, :]
                    pool.wait_ge(rot_done, at_round(b, 2 * NF, n + 1))
                    nc.gpsimd.tensor_tensor(rot[:, n % 2, :], rot[:, n % 2, :], cos_sin[:, 1, :], ALU.mult)\
                        .then_inc(sin_done, 1)
                    pool.wait_ge(sin_done, at_round(b, 2 * NF, n + 1))
                    pool.wait_ge(cos_done, at_round(b, 2 * NF, n + 1))
                    nc.gpsimd.tensor_tensor(dst, dst, rot[:, n % 2, :], ALU.add).then_inc(rope_done, 1)

            def zero_v(b):
                pool.wait_ge(split_done, at_round(b, 2 * NF, 2 * NF))
                pool.nop(nofuse=True)
                pool.wait_ge(kg_done, b + 1)
                pool.nop(nofuse=True)
                nc.gpsimd.memset(v_odd[:, :, :].rearrange("p t (c u d) -> p (t c) u d", u=2, d=HD)[:, :, 0, :], 0.0)\
                    .then_inc(v_zeroed, 1)

            def ln2(b, t):
                rsqrt(b, t, mv2, ve2, rstd2, mv2_done, ve2_done, rstd2_done)
                if t >= NT - 2:
                    return
                pool.wait_ge(rstd2_done, at_round(b, NT, t + 1))
                pool.nop(nofuse=True)
                nc.gpsimd.tensor_scalar(xn[:, t, :], x_res[:, t, :], mv2[:, t, 0:1], rstd2[:, t:t + 1],
                                        ALU.subtract, ALU.mult).then_inc(xn2_done, 1)

            def attention(b):
                def spread_rinv(i):
                    pool.wait_ge(rinv_done, at_round(b, NT, i + 1))
                    if i:
                        pool.wait_ge(pv_done, at_round(b, UNITS, GROUPS * i))
                    pool.nop(nofuse=True)
                    nc.gpsimd.tensor_copy(rinv_wide[:, :, :],
                                          rinv[:, :].unsqueeze(2).broadcast_to([P, HEADS, HD]))\
                        .then_inc(rinv_spread, 1)

                def pack_global(n):
                    pool.wait_ge(exp_done, at_round(b, UNITS, n + 1))
                    pool.nop(nofuse=True)
                    nc.gpsimd.tensor_copy(Pg[:, n % SM_RING, :].rearrange("p (c j) -> p c j", j=NGLOB),
                                          Sm[:, n % SM_RING, :, KEYS:COLS]).then_inc(pg_done, 1)

                def place_global(n):
                    i, g, m = n // GROUPS, n % GROUPS, n - SM_RING
                    if n == 2 * GROUPS:
                        pool.wait_ge(gs_done, at_round(b, 1, 1))
                    if m >= 2 * GROUPS:
                        pool.wait_ge(pg_done, at_round(b, FAR, m - 2 * GROUPS + 1))
                    pool.nop(nofuse=True)
                    nc.gpsimd.tensor_copy(unit_scores(n, KEYS, COLS), Gs[:, i - 2, g * UH:(g + 1) * UH, :])\
                        .then_inc(gs_placed, 1)

                for n in range(STEPS):
                    if 2 * GROUPS <= n + 1 < UNITS:
                        place_global(n + 1)
                    if (i := tile_at(n, SPREAD_LAG)) is not None:
                        spread_rinv(i)
                    if 2 * GROUPS <= n - 1 < UNITS:
                        pack_global(n - 1)
                    if (t := tile_at(n, RES_LAG + 1)) is not None:
                        ln2(b, t)
                ln2(b, NT - 1)

            nc.gpsimd.memset(v_even[:, :, :].rearrange("p t (c u d) -> p (t c) u d", u=2, d=HD)[:, :, 1, :], 0.0)\
                .then_inc(v_set, 1)
            pool.wait_ge(consts_loaded, 16)
            ln1(0)
            pool.wait_ge(attn_loaded, 16 * N_CONST)
            rope(0)
            zero_v(0)
            attention(0)
            with pool.Fori(1, NB) as b:
                ln1(b)
                rope(b)
                zero_v(b)
                attention(b)



def rope_tables(np):
    inv_freq = (np.float32(1.0) / np.float32(10000.0)
                ** (np.arange(0, HD, 2, dtype=np.float32) / np.float32(HD))).astype(np.float32)
    freqs = np.outer(np.arange(SEQ, dtype=np.float32), inv_freq).astype(np.float32)
    emb = np.concatenate([freqs, freqs], -1)
    sign = np.where(np.arange(HD) % 2 == 0, -1.0, 1.0).astype(np.float32)
    cos = np.tile(np.cos(emb).T, (HPT, 1))
    sin = np.tile((np.sin(emb) * sign).T, (HPT, 1))
    return np.ascontiguousarray(np.stack([cos, sin], 1).astype(np.float32))


def masks(np):
    qi, kj = np.arange(P)[:, None], np.arange(P)[None, :]
    before, own = np.where(kj >= qi, 0.0, FAR_OFF), np.where(kj <= qi, 0.0, FAR_OFF)
    before_1 = np.where((kj >= qi) | (kj < NGLOB), 0.0, FAR_OFF)
    window = np.stack([np.concatenate([before, own], 1), np.concatenate([before_1, own], 1)], 1).astype(np.float32)
    rows = np.arange(P)
    headmask = np.where(rows[:, None] // HD == np.arange(HPT)[None, :], -SCALE, 0.0).astype(np.float32)
    minus_half = np.full((P, 1), -0.5, np.float32)
    pick = np.zeros((P, UH * NGLOB), np.float32)
    pick[:NGLOB] = np.tile(np.eye(NGLOB, dtype=np.float32), (1, UH))
    vg = np.zeros((P, 2, UH, 2), np.float32)
    for unit in range(2):
        vg[:UH * NGLOB, unit, :, unit] = np.arange(UH * NGLOB)[:, None] // NGLOB == np.arange(UH)[None, :]
    small = np.concatenate([np.eye(P, dtype=np.float32), headmask,
                            minus_half, pick, vg.reshape(P, -1)], 1).astype(np.float32)
    return np.ascontiguousarray(window), np.ascontiguousarray(small)


def kernel(**inputs):
    import numpy as np
    import concourse.bacc as bacc
    from concourse.bass_utils import run_bass_kernel_spmd

    given = {n: np.asarray(a) for n, a in inputs.items()}

    def tiled(a):
        return np.ascontiguousarray(a.reshape(-1, P, a.shape[-1]).transpose(1, 0, 2))

    heads = np.arange(HEADS).reshape(NF, 2, UH).transpose(0, 2, 1).reshape(-1)
    order = (heads[:, None] * HD + np.arange(HD)[None, :]).reshape(-1)
    qkv = given["L0_attn_qkv_w"]
    qkv = np.concatenate([qkv[:2 * EMB], qkv[2 * EMB:][order]], 0)
    ffn_w = np.concatenate([tiled(given[f"L0_ffn_{n}_w"].T).reshape(P, -1) for n in ("w1", "w2", "h1", "h2", "w3")], 1)
    ffn_s = np.stack([given[f"L0_ffn_{n}_s"].reshape(NH, P).T for n in ("w1", "w2", "h1", "h2")], 1)
    window, small = masks(np)
    arrays = {
        "x": given["L0_attn_x"], "qkvT": tiled(qkv.T), "outT": tiled(given["L0_attn_out_w"].T[order]),
        "ffn_w": ffn_w, "ffn_s": ffn_s, "s3row": given["L0_ffn_w3_s"].reshape(1, EMB),
        "rope": rope_tables(np), "mask": window, "small": small,
    }
    nc = bacc.Bacc("TRN2", target_bir_lowering=False, num_devices=1)
    feed, args = {}, []
    for name, a in arrays.items():
        feed[f"in_{name}"] = np.ascontiguousarray(a)
        args.append(nc.dram_tensor(f"in_{name}", a.shape, mybir.dt.from_np(a.dtype), kind="ExternalInput").ap())
    args.append(nc.dram_tensor("y", (NB, SEQ, EMB), F32, kind="ExternalOutput").ap())
    layer_kernel(nc, *args)
    result = run_bass_kernel_spmd(nc, [feed], core_ids=[0])
    return result.results[0]["y"]
```
